# Optimizing a Trainium2 kernel written in Bass

```python
import numpy as np
import jax
import jax.numpy as jnp

def _softmax(x, axis=-1):
    return jax.nn.softmax(x, axis=axis)

def _gelu(x):
    return jax.nn.gelu(x, approximate=True)

def _silu(x):
    return jax.nn.silu(x)

def _sigmoid(x):
    return jax.nn.sigmoid(x)

def _layernorm(x, axis=-1, eps=1e-05):
    m = jnp.mean(x, axis=axis, keepdims=True)
    v = jnp.var(x, axis=axis, keepdims=True)
    return (x - m) / jnp.sqrt(v + eps)

def _scatter_add(tgt, idx, src, axis=0):
    return tgt.at[idx].add(src)

def _segment_sum(src, seg, n):
    return jax.ops.segment_sum(src, seg, n)
kernel_name = 'mk_sandwich_d1_jaxref_r4_a9b903'

def setup_inputs(seed: int=0):
    np.random.seed(seed)
    _w = jnp.asarray

    def _L0_attn_setup():
        import jax, jax.numpy as jnp
        import numpy as np
        N_HEADS = 16
        WINDOW = 64
        GLOBAL_IDX = np.array([0])

        def _global_local_mask(seq_len):
            i = jnp.arange(seq_len)[:, None]
            j = jnp.arange(seq_len)[None, :]
            g = jnp.asarray(GLOBAL_IDX)
            row_global = jnp.isin(jnp.arange(seq_len), g)
            allowed = (jnp.abs(i - j) <= WINDOW) | row_global[:, None] | row_global[None, :]
            return allowed
        key = jax.random.key(seed)
        ks = jax.random.split(key, 9)
        B, S, D = (1, 512, 256)
        w = 0.02
        return {'x': jax.random.normal(ks[0], (B, S, D), jnp.float32), 'Wq': jax.random.normal(ks[1], (D, D), jnp.float32) * w, 'bq': jnp.zeros((D,), jnp.float32), 'Wk': jax.random.normal(ks[2], (D, D), jnp.float32) * w, 'bk': jnp.zeros((D,), jnp.float32), 'Wv': jax.random.normal(ks[3], (D, D), jnp.float32) * w, 'bv': jnp.zeros((D,), jnp.float32), 'Wo': jax.random.normal(ks[4], (D, D), jnp.float32) * w, 'bo': jnp.zeros((D,), jnp.float32)}
    _L0_attn_in = _L0_attn_setup()

    def _L0_ffn_setup():
        import jax, jax.numpy as jnp
        import numpy as np
        B, N, D = (4, 512, 256)
        SPARSITY = 0.01
        key = jax.random.key(seed)
        k1, k2, k3 = jax.random.split(key, 3)
        x = jax.random.normal(k1, (B, N, D), dtype=jnp.float32)
        spatial = jax.random.normal(k2, (D, D), dtype=jnp.float32) * 0.02
        freq = jnp.fft.fft(spatial, axis=-1)
        k = int(D * SPARSITY)
        mag = jnp.abs(freq)
        kth = jax.lax.top_k(mag, k)[0][:, -1:]
        w_sparse = jnp.where(mag >= kth, freq, 0.0 + 0j)
        bias = jax.random.normal(k3, (D,), dtype=jnp.float32) * 0.01
        return {'x': x, 'w_freq_real': jnp.real(w_sparse).astype(jnp.float32), 'w_freq_imag': jnp.imag(w_sparse).astype(jnp.float32), 'bias': bias}
    _L0_ffn_in = _L0_ffn_setup()
    _d = {'L0_attn_x': _L0_attn_in['x'], 'L0_attn_Wq': _L0_attn_in['Wq'], 'L0_attn_bq': _L0_attn_in['bq'], 'L0_attn_Wk': _L0_attn_in['Wk'], 'L0_attn_bk': _L0_attn_in['bk'], 'L0_attn_Wv': _L0_attn_in['Wv'], 'L0_attn_bv': _L0_attn_in['bv'], 'L0_attn_Wo': _L0_attn_in['Wo'], 'L0_attn_bo': _L0_attn_in['bo'], 'L0_ffn_w_freq_real': _L0_ffn_in['w_freq_real'], 'L0_ffn_w_freq_imag': _L0_ffn_in['w_freq_imag'], 'L0_ffn_bias': _L0_ffn_in['bias']}
    _x0 = _d['L0_attn_x']
    _d['L0_attn_x'] = jax.random.normal(jax.random.fold_in(jax.random.key(seed), 1), (1, 4096, 256), dtype=_x0.dtype)
    del _x0
    return _d

def reference(L0_attn_x, L0_attn_Wq, L0_attn_bq, L0_attn_Wk, L0_attn_bk, L0_attn_Wv, L0_attn_bv, L0_attn_Wo, L0_attn_bo, L0_ffn_w_freq_real, L0_ffn_w_freq_imag, L0_ffn_bias):

    def _L0_attn_ref(x, Wq, bq, Wk, bk, Wv, bv, Wo, bo):
        import jax, jax.numpy as jnp
        import numpy as np
        N_HEADS = 16
        WINDOW = 64
        GLOBAL_IDX = np.array([0])

        def _global_local_mask(seq_len):
            i = jnp.arange(seq_len)[:, None]
            j = jnp.arange(seq_len)[None, :]
            g = jnp.asarray(GLOBAL_IDX)
            row_global = jnp.isin(jnp.arange(seq_len), g)
            allowed = (jnp.abs(i - j) <= WINDOW) | row_global[:, None] | row_global[None, :]
            return allowed
        B, S, D = x.shape
        H = N_HEADS
        Dh = D // H
        scale = Dh ** (-0.5)
        q = (x @ Wq + bq).reshape(B, S, H, Dh)
        k = (x @ Wk + bk).reshape(B, S, H, Dh)
        v = (x @ Wv + bv).reshape(B, S, H, Dh)
        scores = jnp.einsum('bqhd,bkhd->bhqk', q, k) * scale
        allowed = _global_local_mask(S)
        scores = jnp.where(allowed[None, None], scores, -jnp.inf)
        attn = jax.nn.softmax(scores, axis=-1)
        out = jnp.einsum('bhqk,bkhd->bqhd', attn, v).reshape(B, S, D)
        return out @ Wo + bo

    def _L0_ffn_ref(x, w_freq_real, w_freq_imag, bias):
        import jax, jax.numpy as jnp
        import numpy as np
        B, N, D = (4, 512, 256)
        SPARSITY = 0.01
        w = jax.lax.complex(w_freq_real, w_freq_imag)
        x_freq = jnp.fft.fft(x, axis=-1)
        y_freq = jnp.einsum('bnd,do->bno', x_freq, w)
        y = jnp.real(jnp.fft.ifft(y_freq, axis=-1))
        return y + bias
    x = L0_attn_x
    x = x + _layernorm(_L0_attn_ref(_layernorm(x, axis=-1), L0_attn_Wq, L0_attn_bq, L0_attn_Wk, L0_attn_bk, L0_attn_Wv, L0_attn_bv, L0_attn_Wo, L0_attn_bo), axis=-1)
    x = x + _layernorm(_L0_ffn_ref(_layernorm(x, axis=-1), L0_ffn_w_freq_real, L0_ffn_w_freq_imag, L0_ffn_bias), axis=-1)
    return x

_drawn_inputs = setup_inputs


def setup_inputs(seed=0):
    import zlib

    import numpy as np

    out = dict(_drawn_inputs(seed))
    spreads = {'L0_attn_bq': (0.0, 0.8),
     'L0_attn_bk': (0.0, 0.8),
     'L0_attn_bv': (0.0, 0.1),
     'L0_attn_bo': (0.0, 0.1)}
    factors = {'L0_attn_Wq': 7.05, 'L0_attn_Wk': 6.71, 'L0_ffn_bias': 7.063}
    for name, (base, spread) in spreads.items():
        noise = np.random.default_rng([zlib.crc32(name.encode()), seed]).standard_normal(out[name].shape)
        drawn = base * np.exp(spread * noise) if base else spread * noise
        out[name] = jnp.asarray(drawn.astype(out[name].dtype))
    for name, factor in factors.items():
        out[name] = (out[name] * factor).astype(out[name].dtype)
    return out
```

```python
from contextlib import ExitStack

import numpy as np

import concourse.bass as bass
from concourse import mybir

F32 = mybir.dt.float32
BF16 = mybir.dt.bfloat16
ALU = mybir.AluOpType
ACT = mybir.ActivationFunctionType
AX = mybir.AxisListType

S, D, H = 4096, 256, 16
DH = D // H
DV = DH + 1
WIN = 64
P = 128
EPS = 1e-5
NEG = -1e30
SCALE = DH ** -0.5
DC = D // P
NT = S // P
SP_ = S + 2 * WIN
C1 = 512
N1 = S // C1
B1 = C1 // P
C2 = 256
NF = S // C2
BF = C2 // P
KF = C2 + 2 * WIN
RING = 4
BODY = RING * BF
LEAD = 4
AW = 3 * WIN
NG = 4
QPARTS = (0, 0, 0, 1, 1, 2)
KPARTS = (0, 1, 2, 0, 1, 0)
R_PROD = 16 * len(QPARTS)
R_PAD = R_PROD
R_MAX = R_PROD + 1
K_MAXPASS = R_PAD + 1
K_PROB = R_MAX + 2

S_PV = 2
S_T1 = NG + S_PV
S_T2 = S_T1 + 1
S_WO = S_T1 + 2
S_T3 = S_T1 + 4
S_FF = S_T1 + 5
S_END = S_T1 + 7


def build(nc, x, Wq, bq, Wk, bk, Wv, bv, Wo, bo, w_re, w_im, ff_bias, ident_d, mask_d, krows_d,
          cos_d, sin_d, out):
    q_parts = nc.dram_tensor("q_parts", [3, D, S], BF16, kind="Internal").ap()
    k_parts = nc.dram_tensor("k_parts", [3, D, SP_], BF16, kind="Internal").ap()
    krows_b = nc.dram_tensor("krows_b", [3, SP_], BF16, kind="Internal").ap()
    v_rows = nc.dram_tensor("v_rows", [SP_, H * DV], F32, kind="Internal").ap()

    ctx = ExitStack()
    with ctx:
        def sb(name, shape, dt=F32):
            return ctx.enter_context(nc.sbuf_tensor(name, shape, dt))

        def sem(name):
            return ctx.enter_context(nc.semaphore(name))

        ident = sb("ident", [P, P])
        ident_b = sb("ident_b", [P, P], BF16)
        mask_f = sb("mask_f", [P, 2 * AW])
        mask_b = sb("mask_b", [P, 2 * AW], BF16)
        wq, wk, wv, wo = (sb(n, [P, DC, D]) for n in ("wq", "wk", "wv", "wo"))
        mff = sb("mff", [P, DC, D])
        bqk = sb("bqk", [P, 2, DC])
        bv_all, bo_all, bf_all = (sb(n, [P, D]) for n in ("bv_all", "bo_all", "bf_all"))
        minus_half = sb("minus_half", [P, B1])
        psA = ctx.enter_context(nc.psum_tensor("psA", [P, 2, 512], F32))
        psB = [ctx.enter_context(nc.psum_tensor(f"psB{i}", [P, 512], F32)) for i in range(2)]
        psV = ctx.enter_context(nc.psum_tensor("psV", [P, 512], F32))
        psT = ctx.enter_context(nc.psum_tensor("psT", [P, 512], F32))
        psX = ctx.enter_context(nc.psum_tensor("psX", [P, 512], F32))
        psY = ctx.enter_context(nc.psum_tensor("psY", [P, 512], F32))

        s0 = sb("s0", [P, NT + 1, H])
        b = dict(locals())
        stage0(nc, b)
        with ExitStack() as own:
            stage1(nc, own, b)
        with ExitStack() as own:
            stage2(nc, own, b)
        with ExitStack() as own:
            stage3(nc, own, b)


def stage0(nc, b):
    with ExitStack() as own:
        def sb(name, shape):
            return own.enter_context(nc.sbuf_tensor(name, shape, F32))

        wre, wim, cosm, sinm = (sb(n, [P, DC, D]) for n in ("wre", "wim", "cosm", "sinm"))
        nsin = sb("nsin", [P, DC, D])
        grT, giT = sb("grT", [P, DC, D]), sb("giT", [P, DC, D])
        zb = own.enter_context(nc.sbuf_tensor("zb", [P, 3 * DC * WIN], BF16))
        zf = sb("zf", [WIN, H * DV])
        krows = sb("krows", [3, SP_])
        krows_h = own.enter_context(nc.sbuf_tensor("krows_h", [3, SP_], BF16))
        weights_in, consts_in = (own.enter_context(nc.semaphore(n)) for n in ("weights_in", "consts_in"))
        pads_out, zeros_set, const_set, nsin_set, g_done, g_copied, m_done, m_set = (
            own.enter_context(nc.semaphore(n)) for n in (
                "pads_out", "zeros_set", "const_set", "nsin_set", "g_done", "g_copied", "m_done", "m_set"))
        block = own.enter_context(nc.Block())
        rows = "(c p) n -> p c n"

        @block.sync
        def _(sp):
            for dst, src in ((wre, b["w_re"]), (wim, b["w_im"]), (cosm, b["cos_d"]), (sinm, b["sin_d"])):
                sp.dma_start(dst[:, :, :], src.rearrange(rows, p=P)).then_inc(weights_in, 16)
            sp.dma_start(b["ident"][:, :], b["ident_d"]).then_inc(consts_in, 16)
            sp.dma_start(krows[:, :], b["krows_d"]).then_inc(consts_in, 16)
            for i in range(2):
                sp.dma_start(b["mask_f"][:, i * AW:(i + 1) * AW], b["mask_d"]).then_inc(consts_in, 16)
            for i, src in enumerate((b["bq"], b["bk"])):
                for c in range(DC):
                    sp.dma_start(b["bqk"][:, i, c:c + 1], src[c * P:(c + 1) * P].rearrange("(p a) -> p a", a=1))\
                        .then_inc(consts_in, 16)
            for dst, src in ((b["wq"], b["Wq"]), (b["wk"], b["Wk"]), (b["wv"], b["Wv"]), (b["wo"], b["Wo"])):
                sp.dma_start(dst[:, :, :], src.rearrange(rows, p=P)).then_inc(consts_in, 16)
            for dst, src in ((b["bv_all"], b["bv"]), (b["bo_all"], b["bo"]), (b["bf_all"], b["ff_bias"])):
                sp.dma_start(dst[:, :], src.rearrange("(a n) -> a n", a=1).broadcast_to([P, D])).then_inc(consts_in, 16)
            sp.wait_ge(zeros_set, 2)
            for at in (0, WIN + S):
                sp.dma_start(b["k_parts"][:, :, at:at + WIN].rearrange("t (c p) n -> p (t c) n", p=P),
                             zb[:, :].rearrange("p (t n) -> p t n", n=WIN)).then_inc(pads_out, 16)
                sp.dma_start(b["v_rows"][at:at + WIN, :], zf[:, :]).then_inc(pads_out, 16)
            sp.wait_ge(nsin_set, 5)
            sp.dma_start(b["krows_b"], krows_h[:, :]).then_inc(pads_out, 16)
            sp.wait_ge(pads_out, 16 * 5)
            sp.wait_ge(consts_in, 16 * 15)

        @block.gpsimd
        def _(pool):
            nc.gpsimd.memset(b["minus_half"][:, :], -0.5).then_inc(const_set, 1)
            pool.wait_ge(const_set, 1)

        @block.vector
        def _(dve):
            nc.vector.memset(zb[:, :], 0.0).then_inc(zeros_set, 1)
            nc.vector.memset(zf[:, :], 0.0).then_inc(zeros_set, 1)
            dve.wait_ge(weights_in, 16 * 4)
            nc.vector.tensor_scalar(nsin[:, :, :], sinm[:, :, :], -1.0, None, ALU.mult).then_inc(nsin_set, 1)
            dve.wait_ge(consts_in, 16 * 15)
            nc.vector.tensor_copy(b["ident_b"][:, :], b["ident"][:, :]).then_inc(nsin_set, 1)
            nc.vector.tensor_copy(b["mask_b"][:, :], b["mask_f"][:, :]).then_inc(nsin_set, 1)
            nc.vector.tensor_scalar(b["bqk"][:, 0, :], b["bqk"][:, 0, :], SCALE, None, ALU.mult).then_inc(nsin_set, 1)
            nc.vector.tensor_copy(krows_h[:, :], krows[:, :]).then_inc(nsin_set, 1)
            for i, (ps, dst) in enumerate(((b["psB"][0], grT), (b["psB"][1], giT))):
                dve.wait_ge(g_done, i + 1)
                nc.vector.tensor_copy(dst[:, :, :].rearrange("p c n -> p (c n)"), ps[:, :]).then_inc(g_copied, 1)
            dve.wait_ge(m_done, 1)
            nc.vector.tensor_scalar(b["mff"][:, :, :].rearrange("p c n -> p (c n)"), b["psT"][:, :], 1.0 / D, None,
                                    ALU.mult).then_inc(m_set, 1)
            dve.wait_ge(nsin_set, 5)
            dve.wait_ge(m_set, 1)

        @block.tensor
        def _(pe):
            pe.wait_ge(weights_in, 16 * 4)
            pe.wait_ge(nsin_set, 1)
            for ps, terms in ((b["psB"][0], ((wre, cosm), (wim, sinm))), (b["psB"][1], ((wim, cosm), (wre, nsin)))):
                for o in range(DC):
                    for i, (w, f) in enumerate(terms):
                        for c in range(DC):
                            mm = nc.tensor.matmul(ps[:, o * D:(o + 1) * D], w[:, c, o * P:(o + 1) * P], f[:, c, :],
                                                  start=(i + c == 0), stop=(i == 1 and c == DC - 1))
                mm.then_inc(g_done, 1)
            pe.wait_ge(g_copied, 2)
            for o in range(DC):
                for i, (g, f) in enumerate(((grT, cosm), (giT, nsin))):
                    for c in range(DC):
                        mm = nc.tensor.matmul(b["psT"][:, o * D:(o + 1) * D], g[:, c, o * P:(o + 1) * P], f[:, c, :],
                                              start=(i + c == 0), stop=(i == 1 and c == DC - 1))
            mm.then_inc(m_done, 1)


def stage1(nc, own, b):
    def sb(name, shape, dt=F32):
        return own.enter_context(nc.sbuf_tensor(name, shape, dt))

    xc = sb("xc", [P, 2, B1, D])
    hc = sb("hc", [P, 2, B1, D])
    hT = sb("hT", [P, 2, DC, C1])
    full = sb("full", [P, 2, DC, C1])
    left = sb("left", [P, 2, DC, C1])
    part = sb("part", [P, 2, 3, DC, C1], BF16)
    vrow = sb("vrow", [P, 2, B1, H, DV])
    bv2 = sb("bv2", [P, 2, D])
    st1 = sb("st1", [P, B1, 6])
    mv1 = sb("mv1", [P, B1, 2])
    ve1 = sb("ve1", [P, B1])
    rs1 = sb("rs1", [P, B1])
    CREDIT = {"h_done": 2, "turned": 2, "hT_copied": 1, "part1_done": 2, "left_done": 2,
              "part3_done": 2, "v_done": 4, "v_copied": 2}
    s = {n: own.enter_context(nc.semaphore(n)) for n in (
        "stats_done", "aggr_done", "var_done", "rstd_done", "h_done", "turned", "hT_copied", "qk_done",
        "v_done", "part1_done", "left_done", "part2_done", "part3_done", "v_copied", "ones_set", "passed")}
    x_in = [own.enter_context(nc.semaphore(f"x_in{i}")) for i in range(2)]
    qk_out = [own.enter_context(nc.semaphore(f"qk_out{i}")) for i in range(2)]
    v_out = [own.enter_context(nc.semaphore(f"v_out{i}")) for i in range(2)]
    psQK = [[b["psB"][0], b["psB"][1]], [b["psX"], b["psY"]]]
    psVV = [b["psV"], b["psT"]]
    block = own.enter_context(nc.Block())
    PAIRS = N1 // 2

    def after(eng, name, n):
        eng.wait_ge(s[name], n + CREDIT.get(name, 0))

    def apart(eng):
        eng.sem_inc(s["passed"], 1)

    def chunks(eng, body):
        with eng.Fori(0, PAIRS - 1) as i:
            for par in range(2):
                body(i * 2 + par, par, i, False)
        for par in range(2):
            body(N1 - 2 + par, par, PAIRS - 1, True)

    @block.sync
    def _(sp):
        for w in range(2):
            sp.sem_inc(qk_out[w], 48)
            sp.sem_inc(v_out[w], 16)
        for name, n in CREDIT.items():
            sp.sem_inc(s[name], n)

        def load(c, par):
            after(sp, "h_done", c - 1)
            sp.dma_start(xc[:, par, :, :],
                         b["x"][0, bass.ds(c * C1, C1), :].rearrange("(j p) d -> p j d", p=P)).then_inc(x_in[par], 16)

        def body(c, par, use, last):
            if not last:
                load(c + 2, par)
            for w, (dst, pad) in enumerate(((b["q_parts"], 0), (b["k_parts"], WIN))):
                after(sp, "part3_done", c * 2 + w + 1)
                for t in range(3):
                    sp.dma_start(dst[t, :, bass.ds(c * C1 + pad, C1)].rearrange("(o p) n -> p o n", p=P),
                                 part[:, w, t, :, :]).then_inc(qk_out[w], 16)
            after(sp, "v_copied", c * 2 + 2)
            sp.dma_start(b["v_rows"][bass.ds(c * C1 + WIN, C1), :].rearrange("(j p) n -> p j n", p=P),
                         vrow[:, par, :, :, :].rearrange("p j h d -> p j (h d)")).then_inc(v_out[par], 16)

        load(0, 0)
        load(1, 1)
        chunks(sp, body)
        for w in range(2):
            sp.wait_ge(v_out[w], 16 * (PAIRS + 1))
            sp.wait_ge(qk_out[w], 48 * (N1 + 1))

    @block.vector
    def _(dve):
        ones = vrow[:, :, :, :, DH:DV].rearrange("p a j h d -> p (a j h) d")
        nc.vector.memset(ones, 1.0).then_inc(s["ones_set"], 1)
        for j in range(2):
            nc.vector.tensor_copy(bv2[:, j, :], b["bv_all"][:, :]).then_inc(s["ones_set"], 1)
        dve.wait_ge(s["ones_set"], 3)

        def norm(c, par, use):
            dve.wait_ge(x_in[par], use * 16 + 16)
            for j in range(B1):
                nc.vector.bn_stats(st1[:, j, :], xc[:, par, j, :]).then_inc(s["stats_done"], 1)
            for j in range(B1):
                after(dve, "stats_done", c * B1 + j + 1)
                apart(dve)
                nc.vector.bn_aggr(mv1[:, j, :], st1[:, j, :]).then_inc(s["aggr_done"], 1)
            after(dve, "aggr_done", c * B1 + B1)
            nc.vector.tensor_scalar(ve1[:, :], mv1[:, :, 1], EPS, None, ALU.add).then_inc(s["var_done"], 1)
            after(dve, "rstd_done", c + 1)
            after(dve, "turned", c - 1)
            for j in range(B1):
                op = nc.vector.tensor_scalar(hc[:, par, j, :], xc[:, par, j, :], mv1[:, j, 0:1], rs1[:, j:j + 1],
                                             ALU.subtract, ALU.mult)
            op.then_inc(s["h_done"], 1)
            after(dve, "h_done", c + 1)

        def body(c, par, use, last):
            if not (last and par == 1):
                norm(c + 1, 1 - par, use + par)
            for w in range(2):
                after(dve, "part1_done", c * 2 + w + 1)
                after(dve, "part3_done", c * 2 + w - 1)
                nc.vector.tensor_tensor(left[:, w], full[:, w], part[:, w, 0], ALU.subtract).then_inc(s["left_done"], 1)
                after(dve, "left_done", c * 2 + w + 1)
                nc.vector.tensor_copy(part[:, w, 1], left[:, w]).then_inc(s["part2_done"], 1)
            dve.wait_ge(v_out[par], 16 * use + 16)
            for half in range(2):
                after(dve, "v_done", c * 2 + half + 1)
                nc.vector.tensor_tensor(
                    vrow[:, par, 2 * half:2 * half + 2, :, 0:DH].rearrange("p j h d -> p (j h) d"),
                    psVV[half][:, :].rearrange("p (g d) -> p g d", d=DH),
                    bv2[:, :, :].rearrange("p j (h d) -> p (j h) d", d=DH), ALU.add).then_inc(s["v_copied"], 1)

        norm(0, 0, 0)
        chunks(dve, body)

    @block.gpsimd
    def _(pool):
        def rstd(c):
            after(pool, "var_done", c + 1)
            nc.gpsimd.tensor_tensor(rs1[:, :], ve1[:, :], b["minus_half"][:, :], ALU.pow).then_inc(s["rstd_done"], 1)

        def body(c, par, use, last):
            if not (last and par == 1):
                rstd(c + 1)
            for w in range(2):
                after(pool, "part2_done", c * 2 + w + 1)
                nc.gpsimd.tensor_tensor(part[:, w, 2], left[:, w], part[:, w, 1], ALU.subtract)\
                    .then_inc(s["part3_done"], 1)

        rstd(0)
        chunks(pool, body)

    @block.scalar
    def _(act):
        def hT_copy(c, par):
            after(act, "turned", c + 1)
            after(act, "v_done", c * 2 - 2)
            nc.scalar.copy(hT[:, par, :, :], b["psA"][:, :, :]).then_inc(s["hT_copied"], 1)

        def body(c, par, use, last):
            if not (last and par == 1):
                hT_copy(c + 1, 1 - par)
            for w in range(2):
                act.wait_ge(s["qk_done"], c * 2 + w + 1)
                after(act, "left_done", c * 2 + w - 1)
                act.wait_ge(qk_out[w], 48 * c + 48)
                for o in range(DC):
                    for dst in (full[:, w, o, :], part[:, w, 0, o, :]):
                        op = nc.scalar.activation(dst, psQK[w][o][:, :], ACT.Identity, bias=b["bqk"][:, w, o:o + 1],
                                                  scale=(SCALE, 1.0)[w])
                op.then_inc(s["part1_done"], 1)

        hT_copy(0, 0)
        chunks(act, body)

    @block.tensor
    def _(pe):
        def turn(c, par):
            after(pe, "h_done", c + 1)
            after(pe, "hT_copied", c)
            for j in range(B1):
                for d in range(DC):
                    op = nc.tensor.transpose(b["psA"][:, d, j * P:(j + 1) * P], hc[:, par, j, d * P:(d + 1) * P],
                                             b["ident"][:, :])
            op.then_inc(s["turned"], 1)

        def body(c, par, use, last):
            if not (last and par == 1):
                turn(c + 1, 1 - par)
            after(pe, "hT_copied", c + 1)
            for w, weight in enumerate((b["wq"], b["wk"])):
                after(pe, "part1_done", c * 2 + w - 1)
                for o in range(DC):
                    for d in range(DC):
                        op = nc.tensor.matmul(psQK[w][o][:, :], weight[:, d, o * P:(o + 1) * P], hT[:, par, d, :],
                                              start=(d == 0), stop=(d == DC - 1))
                op.then_inc(s["qk_done"], 1)
            for half in range(2):
                after(pe, "v_copied", c * 2 + half - 1)
                for j in range(2):
                    t = half * 2 + j
                    for d in range(DC):
                        op = nc.tensor.matmul(psVV[half][:, j * D:(j + 1) * D], hT[:, par, d, t * P:(t + 1) * P],
                                              b["wv"][:, d, :], start=(d == 0), stop=(d == DC - 1))
                op.then_inc(s["v_done"], 1)

        turn(0, 0)
        chunks(pe, body)


def stage2(nc, own, b):
    def sb(name, shape, dt=F32):
        return own.enter_context(nc.sbuf_tensor(name, shape, dt))

    q_st = sb("q_st", [P, RING, H, C2], BF16)
    k_st = sb("k_st", [P, RING, H, KF], BF16)
    v_st = sb("v_st", [P, RING, BF + 1, H, DV])
    k0 = sb("k0", [P, H], BF16)
    q0 = sb("q0", [P, H], BF16)
    v0_all = sb("v0_all", [P, H, DV])
    nmax = sb("nmax", [P, 2, BF, H])
    gsc = sb("gsc", [P, 2, BF, H])
    ngsc = sb("ngsc", [P, BF, H])
    nshift = sb("nshift", [P, BF, H])
    hilo = sb("hilo", [P, 2, BF, 2, H], BF16)
    shift = sb("shift", [P, BF, H])
    earg = sb("earg", [P, 2, BF, H])
    eglob = sb("eglob", [P, RING, BF, H])
    shiftT = sb("shiftT", [2 * H, 2, C2], BF16)
    prob = sb("prob", [P, NG, 4, 2, P])
    gpart = sb("gpart", [P, 2, H, DV])
    oslot = sb("oslot", [P, NG, P])
    osum = sb("osum", [P, 2, H, DV])
    rden = sb("rden", [P, 2, H])
    on = sb("on", [P, 2, D])
    oT = sb("oT", [P, DC, P])
    att = sb("att", [P, 2, D])
    z1 = sb("z1", [P, 2, D])
    xin = sb("xin", [P, 4, D])
    x1 = sb("x1", [P, 4, D])
    h2 = sb("h2", [P, 2, D])
    h2T = sb("h2T", [P, DC, P])
    yff = sb("yff", [P, 2, D])
    z3 = sb("z3", [P, 2, D])
    res = sb("res", [P, 2, D])
    st = sb("st", [P, 3, 2, 6])
    mv = sb("mv", [P, 3, 2, 2])
    ve = sb("ve", [P, 3, 2])
    rs = sb("rs", [P, 3, 2])

    CREDIT = {"a_read": 1, "exp_done": 2, "pv_done": 4, "ov_done": 1, "t1_done": 1, "osum_done": 2,
              "x_read": 1, "wo_done": 1, "ff_done": 1, "y_read": 1, "eg_done": 2, "gp_done": 8}
    s = {n: own.enter_context(nc.semaphore(n)) for n in (
        "a_done",
        "a_read",
        "shift_step",
        "shT_done",
        "eg_done",
        "b_done",
        "exp_done",
        "sel_done",
        "pv_done",
        "ov_done",
        "t1_done",
        "gp_done",
        "osum_done",
        "rden_done", "on_done",
        "t2_done",
        "x_read",
        "wo_done",
        "y_read",
        "stat_done", "aggr_done", "var_done", "rstd_done", "z_done",
        "x1_done", "t3_done", "ff_done", "res_done", "first_rows", "cleared", "passed")}
    frame_in = [own.enter_context(nc.semaphore(f"frame_in{i}")) for i in range(RING)]
    v_in = [own.enter_context(nc.semaphore(f"v_in{i}")) for i in range(RING)]
    x_in = [own.enter_context(nc.semaphore(f"xblock_in{i}")) for i in range(4)]
    shift_in = [own.enter_context(nc.semaphore(f"shift_in{i}")) for i in range(2)]
    out_st = [own.enter_context(nc.semaphore(f"out_st{i}")) for i in range(2)]
    v0_in = own.enter_context(nc.semaphore("v0_in"))
    FRAME_DMAS = len(QPARTS) + len(KPARTS) + 1
    block = own.enter_context(nc.Block())
    BODIES = NT // BODY
    SLOTS = NG * BODY

    def after(eng, name, n):
        eng.wait_ge(s[name], n + CREDIT.get(name, 0))

    def apart(eng):
        eng.sem_inc(s["passed"], 1)

    def bodies(eng, step):
        with eng.Fori(0, BODIES - 1) as i:
            for slot in range(SLOTS + S_END):
                step(slot, i, False)
        for slot in range(SLOTS + S_END):
            step(slot, BODIES - 1, True)

    def main(slot):
        return divmod(slot, NG) if slot < SLOTS else None

    def at(slot, offset):
        k, rest = divmod(slot - offset, NG)
        return k if rest == 0 and 0 <= k < BODY else None

    def ahead(k, last):
        return not last or k + LEAD < BODY

    @block.sync
    def _(sp):
        for name, n in CREDIT.items():
            sp.sem_inc(s[name], n)
        for i in range(2):
            sp.sem_inc(shift_in[i], 32)
            sp.sem_inc(out_st[i], 16)

        def load_frame(f, r):
            for i, t in enumerate(QPARTS):
                sp.dma_start(q_st[16 * i:16 * i + 16, r, :, :],
                             b["q_parts"][t, :, bass.ds(f * C2, C2)].rearrange("(h d) n -> d h n", d=DH))\
                    .then_inc(frame_in[r], 16)
            for i, t in enumerate(KPARTS):
                sp.dma_start(k_st[16 * i:16 * i + 16, r, :, :],
                             b["k_parts"][t, :, bass.ds(f * C2, KF)].rearrange("(h d) n -> d h n", d=DH))\
                    .then_inc(frame_in[r], 16)
            sp.dma_start(k_st[R_PAD:R_MAX + 2, r, :, :],
                         b["krows_b"][:, bass.ds(f * C2, KF)].rearrange("r (a n) -> r a n", a=1)
                         .broadcast_to([3, H, KF])).then_inc(frame_in[r], 16)

        def load_v(f, r):
            sp.dma_start(v_st[:, r, :, :, :].rearrange("p t h d -> p t (h d)"),
                         b["v_rows"][bass.ds(f * C2, (BF + 1) * P), :].rearrange("(t p) n -> p t n", p=P))\
                .then_inc(v_in[r], 16)

        def load_x(n, k):
            sp.dma_start(xin[:, k % 4, :], b["x"][0, bass.ds(n * P, P), :]).then_inc(x_in[k % 4], 16)

        def place_shifts(i, kf):
            after(sp, "shT_done", i * RING + kf + 1)
            for part in range(2):
                sp.dma_start(q_st[R_MAX + part:R_MAX + part + 1, kf % RING, :, :],
                             shiftT[part * H:part * H + H, kf % 2, :]).then_inc(shift_in[kf % 2], 16)

        def step(slot, i, last):
            base = i * BODY
            if main(slot):
                k, g = main(slot)
                if k % 2 == 0 and g == 2:
                    if ahead(k, last) or k == LEAD:
                        place_shifts(i, (k + LEAD) // BF - 1)
            k = at(slot, 5)
            if k is not None and k % BF == BF - 1 and not last:
                after(sp, "b_done", 8 * (base + k) + 8)
                load_frame((i + 1) * RING + k // BF, k // BF)
                after(sp, "pv_done", 4 * (base + k) + 4)
                load_v((i + 1) * RING + k // BF, k // BF)
            k = at(slot, S_WO + 1)
            if k is not None and (not last or k + 4 < BODY):
                after(sp, "x1_done", base + k + 1)
                load_x(base + k + 4, k)
            k = at(slot, S_FF + 1)
            if k is not None:
                after(sp, "res_done", base + k + 1)
                sp.dma_start(b["out"][0, bass.ds((base + k) * P, P), :], res[:, k % 2, :]).then_inc(out_st[k % 2], 16)

        sp.wait_ge(s["cleared"], 1)
        for f in range(RING):
            load_frame(f, f)
            if f == 0:
                sp.dma_start(v0_all[:, :, :].rearrange("p h d -> p (h d)"),
                             b["v_rows"][WIN:WIN + 1, :].broadcast_to([P, H * DV])).then_inc(v0_in, 16)
        for f in range(RING):
            load_v(f, f)
            load_x(f, f)
        place_shifts(0, 0)
        bodies(sp, step)
        for i in range(2):
            sp.wait_ge(out_st[i], 16 * (NT // 2 + 1))

    @block.tensor
    def _(pe):
        def maxima(i, km, g):
            m, use = i * BODY + km, i + km // BODY
            r, j = km // BF % RING, km % BF
            after(pe, "a_read", 4 * m + g)
            if g == 0:
                pe.wait_ge(frame_in[r], 16 * FRAME_DMAS * (use + 1))
                if km == 0:
                    pe.wait_ge(s["first_rows"], 2)
            for bank in range(2):
                nc.tensor.matmul(b["psA"][:, bank, 0:2 * AW], b["ident_b"][:, :], b["mask_b"][:, :], start=True, stop=False)
                for hh in range(2):
                    h = 4 * g + 2 * bank + hh
                    for t in range(2):
                        c = j * P + t * WIN
                        op = nc.tensor.matmul(b["psA"][t * WIN:t * WIN + WIN, bank, hh * AW:hh * AW + AW],
                                              q_st[0:K_MAXPASS, r, h, c:c + WIN], k_st[0:K_MAXPASS, r, h, c:c + AW],
                                              start=False, stop=(hh == 1))
            if g == 0:
                for h in range(H):
                    nc.tensor.matmul(b["psA"][:, 0, 2 * AW + h:2 * AW + h + 1], q_st[0:R_PROD, r, h, j * P:j * P + P],
                                     k0[0:R_PROD, h:h + 1], start=True, stop=True)
                op = query0(r, j)
            if g == 2 and km % BF == 0 and km > 0:
                op = turn_shifts(i, km)
            op.then_inc(s["a_done"], 1)

        def query0(r, j):
            for h in range(H):
                op = nc.tensor.matmul(b["psA"][:, 0, 2 * AW + H + h:2 * AW + H + h + 1],
                                      k_st[0:R_PROD, r, h, j * P:j * P + P], q0[0:R_PROD, h:h + 1],
                                      start=True, stop=True)
            return op

        def turn_shifts(i, km):
            kf = km // BF - 1
            after(pe, "shift_step", 6 * (i * RING + kf) + 4)
            for j in range(BF):
                op = nc.tensor.transpose(
                    b["psA"][0:2 * H, 1, 2 * AW + j * WIN:2 * AW + (j + 1) * WIN].bitcast(BF16),
                    hilo[:, kf % 2, j, :, :].rearrange("p a h -> p (a h)"), b["ident_b"][:, :])
            return op

        def scores(n, k, u):
            r, j = k // BF % RING, k % BF
            after(pe, "exp_done", 8 * n + u - 1)
            for hh in range(2):
                for t in range(2):
                    c = (hh * 2 + t) * P
                    op = nc.tensor.matmul(b["psB"][u % 2][:, c:c + P],
                                          k_st[0:K_PROB, r, 2 * u + hh, (j + t) * P:(j + t + 1) * P],
                                          q_st[0:K_PROB, r, 2 * u + hh, j * P:j * P + P], start=True, stop=True)
            op.then_inc(s["b_done"], 1)

        def values(n, k, g):
            r, j = k // BF % RING, k % BF
            after(pe, "sel_done", 8 * n + 2 * g + 2)
            if g == 0:
                after(pe, "ov_done", n)
            for t in range(2):
                for hq in range(4):
                    op = nc.tensor.matmul(b["psV"][32 * hq:32 * hq + DV, g * P:g * P + P], v_st[:, r, j + t, 4 * g + hq, :],
                                          prob[:, g, hq, t, :], start=(t == 0), stop=(t == 1), skip_group_check=True)
            op.then_inc(s["pv_done"], 1)

        def step(slot, i, last):
            base = i * BODY
            if main(slot):
                k, g = main(slot)
                n = base + k
                if ahead(k, last):
                    maxima(i, k + LEAD, g)
                elif k == LEAD and g == 0:
                    after(pe, "a_read", 4 * NT)
                    query0(RING - 1, BF).then_inc(s["a_done"], 1)
                elif k == LEAD and g == 2:
                    after(pe, "a_read", 4 * NT + 1)
                    turn_shifts(i, k + LEAD).then_inc(s["a_done"], 1)
                if g == 0 and k % BF == 0:
                    pe.wait_ge(shift_in[k // BF % 2], (i * (RING // 2) + k // BF // 2 + 2) * 32)
                    pe.wait_ge(v_in[k // BF], 16 * (i + 1))
                for u in (2 * g, 2 * g + 1):
                    scores(n, k, u)
            if 0 <= slot - S_PV < SLOTS:
                k, g = divmod(slot - S_PV, NG)
                values(base + k, k, g)
            if (k := at(slot, S_T3)) is not None:
                n = base + k
                after(pe, "z_done", 3 * n + 2)
                after(pe, "x_read", 2 * n + 1)
                for c in range(DC):
                    op = nc.tensor.transpose(b["psX"][:, D + c * P:D + c * P + P], h2[:, k % 2, c * P:c * P + P], b["ident"][:, :])
                op.then_inc(s["t3_done"], 1)
            if (k := at(slot, S_FF)) is not None:
                n = base + k
                after(pe, "x_read", 2 * n + 2)
                after(pe, "y_read", 2 * n + 1)
                for c in range(DC):
                    op = nc.tensor.matmul(b["psY"][:, D:2 * D], h2T[:, c, :], b["mff"][:, c, :], start=(c == 0), stop=(c == DC - 1))
                op.then_inc(s["ff_done"], 1)
            if (k := at(slot, S_T1)) is not None:
                n = base + k
                after(pe, "ov_done", n + 1)
                after(pe, "osum_done", n)
                for g in range(NG):
                    op = nc.tensor.transpose(b["psT"][:, g * P:g * P + P], oslot[:, g, :], b["ident"][:, :])
                op.then_inc(s["t1_done"], 1)
            if (k := at(slot, S_T2)) is not None:
                n = base + k
                after(pe, "on_done", n + 1)
                after(pe, "x_read", 2 * n)
                for c in range(DC):
                    op = nc.tensor.transpose(b["psX"][:, c * P:c * P + P], on[:, k % 2, c * P:c * P + P], b["ident"][:, :])
                op.then_inc(s["t2_done"], 1)
            if (k := at(slot, S_WO)) is not None:
                n = base + k
                after(pe, "x_read", 2 * n + 1)
                after(pe, "y_read", 2 * n)
                for c in range(DC):
                    op = nc.tensor.matmul(b["psY"][:, 0:D], oT[:, c, :], b["wo"][:, c, :], start=(c == 0), stop=(c == DC - 1))
                op.then_inc(s["wo_done"], 1)

        for m in range(LEAD):
            for g in range(NG):
                maxima(0, m, g)
        bodies(pe, step)

    @block.vector
    def _(dve):
        def take_maxima(i, km, g):
            m = i * BODY + km
            j, fp = km % BF, km // BF % 2
            after(dve, "a_done", 4 * m + g + 1)
            if g == 0:
                nc.vector.tensor_copy(gsc[:, fp, j, :], b["psA"][:, 0, 2 * AW:2 * AW + H])
                take_query0(m)
            if g == 2 and km % BF == 0 and km > 0:
                copy_shifts(i, km)
            nc.vector.tensor_reduce(out=nmax[:, fp, j, 4 * g:4 * g + 4],
                                    in_=b["psA"][:, :, 0:2 * AW].rearrange("p b (h k) -> p b h k", h=2),
                                    axis=AX.X, op=ALU.max, negate=True).then_inc(s["a_read"], 1)
            if g == NG - 1 and j == BF - 1:
                find_shifts(i, km, fp)

        def take_query0(m):
            return nc.vector.tensor_copy(b["s0"][:, bass.ds(m, 1), :].rearrange("p a h -> p (a h)"),
                                         b["psA"][:, 0, 2 * AW + H:2 * AW + 2 * H])

        def copy_shifts(i, km):
            kf = km // BF - 1
            dve.wait_ge(shift_in[kf % 2], (i * (RING // 2) + kf // 2 + 1) * 32)
            return nc.vector.tensor_copy(shiftT[:, kf % 2, :], b["psA"][0:2 * H, 1, 2 * AW:512].bitcast(BF16))\
                .then_inc(s["shT_done"], 1)

        def find_shifts(i, km, fp):
            f = i * RING + km // BF
            after(dve, "a_read", 4 * (i * BODY + km) + 4)
            nc.vector.tensor_scalar(ngsc[:, :, :], gsc[:, fp], -1.0, None, ALU.mult).then_inc(s["shift_step"], 1)
            after(dve, "shift_step", 6 * f + 1)
            nc.vector.tensor_tensor(nshift[:, :, :], nmax[:, fp], ngsc[:, :, :], ALU.min).then_inc(s["shift_step"], 1)
            after(dve, "shift_step", 6 * f + 2)
            nc.vector.tensor_copy(hilo[:, fp, :, 0, :], nshift[:, :, :]).then_inc(s["shift_step"], 1)
            after(dve, "shift_step", 6 * f + 3)
            nc.vector.tensor_tensor(hilo[:, fp, :, 1, :], nshift[:, :, :], hilo[:, fp, :, 0, :], ALU.subtract)\
                .then_inc(s["shift_step"], 1)
            after(dve, "shift_step", 6 * f + 4)
            nc.vector.tensor_tensor(shift[:, :, :], hilo[:, fp, :, 0, :], hilo[:, fp, :, 1, :], ALU.add)\
                .then_inc(s["shift_step"], 1)
            after(dve, "shift_step", 6 * f + 5)
            after(dve, "eg_done", f - 1)
            nc.vector.tensor_tensor(earg[:, fp], gsc[:, fp], shift[:, :, :], ALU.add).then_inc(s["shift_step"], 1)

        def statistics(n, k, which, rows):
            p = k % 2
            nc.vector.bn_stats(st[:, which, p, :], rows).then_inc(s["stat_done"], 1)
            after(dve, "stat_done", 3 * n + which + 1)
            apart(dve)
            nc.vector.bn_aggr(mv[:, which, p, :], st[:, which, p, :]).then_inc(s["aggr_done"], 1)
            after(dve, "aggr_done", 3 * n + which + 1)
            nc.vector.tensor_scalar(ve[:, which, p:p + 1], mv[:, which, p, 1:2], EPS, None, ALU.add)\
                .then_inc(s["var_done"], 1)

        def normalise(n, k, which, dst, rows):
            p = k % 2
            after(dve, "rstd_done", 3 * n + which + 1)
            nc.vector.tensor_scalar(dst, rows, mv[:, which, p, 0:1], rs[:, which, p:p + 1], ALU.subtract, ALU.mult)\
                .then_inc(s["z_done"], 1)

        def step(slot, i, last):
            base = i * BODY
            if main(slot):
                k, g = main(slot)
                if ahead(k, last):
                    take_maxima(i, k + LEAD, g)
                elif k == LEAD and g == 0:
                    after(dve, "a_done", 4 * NT + 1)
                    take_query0(NT).then_inc(s["a_read"], 1)
                elif k == LEAD and g == 2:
                    after(dve, "a_done", 4 * NT + 2)
                    copy_shifts(i, k + LEAD)
            if (k := at(slot, S_T1)) is not None:
                n, p = base + k, k % 2
                after(dve, "t1_done", n + 1)
                after(dve, "gp_done", n + 1)
                nc.vector.tensor_tensor(osum[:, p], b["psT"][:, :].rearrange("p (h d) -> p h d", h=H)[:, :, 0:DV],
                                        gpart[:, p], ALU.add).then_inc(s["osum_done"], 1)
                after(dve, "osum_done", n + 1)
                nc.vector.reciprocal(rden[:, p, :], osum[:, p, :, DH]).then_inc(s["rden_done"], 1)
                after(dve, "rden_done", n + 1)
                nc.vector.tensor_tensor(on[:, p, :].rearrange("p (h d) -> p h d", h=H), osum[:, p, :, 0:DH],
                                        rden[:, p, :].rearrange("p (h a) -> p h a", a=1).broadcast_to([P, H, DH]),
                                        ALU.mult).then_inc(s["on_done"], 1)
            if (k := at(slot, S_WO)) is not None:
                n, p = base + k, k % 2
                after(dve, "wo_done", n + 1)
                nc.vector.tensor_tensor(att[:, p, :], b["psY"][:, 0:D], b["bo_all"][:, :], ALU.add).then_inc(s["y_read"], 1)
                after(dve, "y_read", 2 * n + 1)
                statistics(n, k, 0, att[:, p, :])
                normalise(n, k, 0, z1[:, p, :], att[:, p, :])
            if (k := at(slot, S_WO + 1)) is not None:
                n, p = base + k, k % 2
                after(dve, "x1_done", n + 1)
                statistics(n, k, 1, x1[:, k % 4, :])
                normalise(n, k, 1, h2[:, p, :], x1[:, k % 4, :])
            if (k := at(slot, S_FF)) is not None:
                n, p = base + k, k % 2
                after(dve, "ff_done", n + 1)
                nc.vector.tensor_tensor(yff[:, p, :], b["psY"][:, D:2 * D], b["bf_all"][:, :], ALU.add).then_inc(s["y_read"], 1)
                after(dve, "y_read", 2 * n + 2)
                statistics(n, k, 2, yff[:, p, :])
                normalise(n, k, 2, z3[:, p, :], yff[:, p, :])

        nc.vector.memset(q_st[R_PROD:P, :, :, :].rearrange("p r h n -> p (r h n)"), 1.0).then_inc(s["cleared"], 1)
        nc.vector.memset(b["psV"][:, :], 0.0)
        dve.wait_ge(frame_in[0], 16 * FRAME_DMAS)
        nc.vector.tensor_copy(k0[0:R_PROD, :], k_st[0:R_PROD, 0, :, WIN]).then_inc(s["first_rows"], 1)
        nc.vector.tensor_copy(q0[0:R_PROD, :], q_st[0:R_PROD, 0, :, 0]).then_inc(s["first_rows"], 1)
        for m in range(LEAD):
            for g in range(NG):
                take_maxima(0, m, g)
        bodies(dve, step)

    @block.scalar
    def _(act):
        def key0(f, kf):
            after(act, "shift_step", 6 * f + 6)
            after(act, "gp_done", 2 * f - 6)
            nc.scalar.activation(eglob[:, kf % RING], earg[:, kf % 2], ACT.Exp).then_inc(s["eg_done"], 1)

        def step(slot, i, last):
            base = i * BODY
            if main(slot):
                k, g = main(slot)
                n = base + k
                for u in (2 * g, 2 * g + 1):
                    act.wait_ge(s["b_done"], 8 * n + u + 1)
                    if u % 2 == 0:
                        after(act, "pv_done", 4 * n + g - 3)
                    nc.scalar.activation(prob[:, g, 2 * (u % 2):2 * (u % 2) + 2, :, :].rearrange("p h t n -> p (h t n)"),
                                         b["psB"][u % 2][:, :], ACT.Exp).then_inc(s["exp_done"], 1)
            if (k := at(slot, 4)) is not None and k % BF == BF - 1 and ahead(k, last):
                key0(i * RING + (k + LEAD) // BF, (k + LEAD) // BF)
            if (k := at(slot, 5)) is not None:
                n = base + k
                after(act, "pv_done", 4 * n + 4)
                after(act, "t1_done", n)
                nc.scalar.copy(oslot[:, :, :].rearrange("p g n -> p (g n)"), b["psV"][:, :]).then_inc(s["ov_done"], 1)
            if (k := at(slot, S_T3)) is not None:
                n = base + k
                after(act, "t3_done", n + 1)
                after(act, "ff_done", n)
                nc.scalar.copy(h2T[:, :, :].rearrange("p c n -> p (c n)"), b["psX"][:, D:2 * D]).then_inc(s["x_read"], 1)
            if (k := at(slot, S_T2)) is not None:
                n = base + k
                after(act, "t2_done", n + 1)
                after(act, "wo_done", n)
                nc.scalar.copy(oT[:, :, :].rearrange("p c n -> p (c n)"), b["psX"][:, 0:D]).then_inc(s["x_read"], 1)

        for f in range(LEAD // BF):
            key0(f, f)
        bodies(act, step)

    @block.gpsimd
    def _(pool):
        def rstd(n, k, which):
            p = k % 2
            after(pool, "var_done", 3 * n + which + 1)
            nc.gpsimd.tensor_tensor(rs[:, which, p:p + 1], ve[:, which, p:p + 1], b["minus_half"][:, 0:1], ALU.pow)\
                .then_inc(s["rstd_done"], 1)

        def step(slot, i, last):
            base = i * BODY
            if main(slot):
                k, g = main(slot)
                n = base + k
                after(pool, "exp_done", 8 * n + 2 * g + 2)
                apart(pool)
                nc.gpsimd.affine_select(out=prob[:, g, :, 0, :], in_=prob[:, g, :, 0, :], pattern=[[0, 4], [-1, P]],
                                        compare_op=ALU.is_ge, fill=0.0, base=0, channel_multiplier=1)\
                    .then_inc(s["sel_done"], 1)
                nc.gpsimd.affine_select(out=prob[:, g, :, 1, :], in_=prob[:, g, :, 1, :], pattern=[[0, 4], [1, P]],
                                        compare_op=ALU.is_ge, fill=0.0, base=0, channel_multiplier=-1)\
                    .then_inc(s["sel_done"], 1)
            if (k := at(slot, 5)) is not None:
                n, p = base + k, k % 2
                after(pool, "eg_done", i * RING + k // BF + 1)
                after(pool, "osum_done", n - 1)
                nc.gpsimd.tensor_tensor(
                    gpart[:, p], v0_all[:, :, :],
                    eglob[:, k // BF, k % BF, :].rearrange("p (h a) -> p h a", a=1).broadcast_to([P, H, DV]),
                    ALU.mult).then_inc(s["gp_done"], 1)
            if (k := at(slot, S_WO)) is not None:
                n, p = base + k, k % 2
                rstd(n, k, 0)
                pool.wait_ge(x_in[k % 4], (i * 2 + k // 4 + 1) * 16)
                after(pool, "z_done", 3 * n + 1)
                nc.gpsimd.tensor_tensor(x1[:, k % 4, :], z1[:, p, :], xin[:, k % 4, :], ALU.add).then_inc(s["x1_done"], 1)
            if (k := at(slot, S_WO + 1)) is not None:
                rstd(base + k, k, 1)
            if (k := at(slot, S_FF)) is not None:
                n, p = base + k, k % 2
                rstd(n, k, 2)
                after(pool, "z_done", 3 * n + 3)
                pool.wait_ge(out_st[p], (i * (BODY // 2) + k // 2 + 1) * 16)
                nc.gpsimd.tensor_tensor(res[:, p, :], z3[:, p, :], x1[:, k % 4, :], ALU.add).then_inc(s["res_done"], 1)

        pool.wait_ge(v0_in, 16)
        bodies(pool, step)


def stage3(nc, own, b):
    def sb(name, shape, dt=F32):
        return own.enter_context(nc.sbuf_tensor(name, shape, dt))

    v_all = sb("v_all", [P, NT + 1, H * DV])
    tile_max = sb("tile_max", [P, H])
    all_max = sb("all_max", [P, H])
    e0 = sb("e0", [P, NT + 1, H])
    own_head = sb("own_head", [H, H, DV])
    od = sb("od", [H, DV])
    rd = sb("rd", [H, 1])
    diag = sb("diag", [H, D])
    one_row = sb("one_row", [H, 1])
    col = sb("col", [P, 2, DC])
    row = sb("row", [1, 6, D])
    xrow = sb("xrow", [1, D])
    st, mv = sb("st_row", [1, 3, 6]), sb("mv_row", [1, 3, 2])
    ve, rs = sb("ve_row", [1, 3]), sb("rs_row", [1, 3])
    s = {n: own.enter_context(nc.semaphore(n)) for n in (
        "v_all_in", "xrow_in", "row_st", "step0", "max_done", "all_max_done", "less_done", "e0_done",
        "pv0_done", "diag_done", "col_done", "col_copied", "row_done", "var0_done", "rstd0_done")}
    block = own.enter_context(nc.Block())

    @block.sync
    def _(sp):
        sp.dma_start(v_all[:, :, :], b["v_rows"].rearrange("(t p) n -> p t n", p=P)).then_inc(s["v_all_in"], 16)
        sp.dma_start(xrow[:, :], b["x"][0, 0:1, :]).then_inc(s["xrow_in"], 16)
        sp.wait_ge(s["row_done"], 3)
        sp.dma_start(b["out"][0, 0:1, :], row[0:1, 5, :]).then_inc(s["row_st"], 16)
        sp.wait_ge(s["row_st"], 16)

    @block.gpsimd
    def _(pool):
        pool.wait_ge(s["max_done"], 1)
        nc.gpsimd.partition_all_reduce(all_max[:, :], tile_max[:, :], P, bass.bass_isa.ReduceOp.max)\
            .then_inc(s["all_max_done"], 1)
        for which in range(3):
            pool.wait_ge(s["var0_done"], which + 1)
            nc.gpsimd.tensor_tensor(rs[0:1, which:which + 1], ve[0:1, which:which + 1], b["minus_half"][0:1, 0:1],
                                    ALU.pow).then_inc(s["rstd0_done"], 1)

    @block.scalar
    def _(act):
        act.wait_ge(s["less_done"], 1)
        nc.scalar.activation(e0[:, :, :], b["s0"][:, :, :], ACT.Exp).then_inc(s["e0_done"], 1)

    @block.tensor
    def _(pe):
        pe.wait_ge(s["e0_done"], 1)
        pe.wait_ge(s["v_all_in"], 16)
        for t in range(NT + 1):
            op = nc.tensor.matmul(b["psB"][0][0:H, 0:H * DV], e0[:, t, :], v_all[:, t, :], start=(t == 0), stop=(t == NT))
        op.then_inc(s["pv0_done"], 1)
        pe.wait_ge(s["diag_done"], 1)
        for c in range(DC):
            op = nc.tensor.matmul(b["psX"][:, c:c + 1], diag[:, c * P:c * P + P], one_row[:, :], start=True, stop=True)
        op.then_inc(s["col_done"], 1)
        for n, (weight, ps) in enumerate(((b["wo"], b["psY"]), (b["mff"], b["psT"]))):
            if n == 1:
                pe.wait_ge(s["row_done"], 2)
                for c in range(DC):
                    op = nc.tensor.matmul(b["psX"][:, c:c + 1], row[0:1, 3, c * P:c * P + P], one_row[0:1, :],
                                          start=True, stop=True)
                op.then_inc(s["col_done"], 1)
            pe.wait_ge(s["col_copied"], n + 1)
            for c in range(DC):
                op = nc.tensor.matmul(ps[0:1, 0:D], col[:, n, c:c + 1], weight[:, c, :], start=(c == 0), stop=(c == DC - 1))
            op.then_inc(s["pv0_done"], 1)

    @block.vector
    def _(dve):
        done = [0]

        def then(op):
            done[0] += 1
            op.then_inc(s["step0"], 1)
            dve.wait_ge(s["step0"], done[0])

        def norm(which, dst, rows, tells=None):
            then(nc.vector.bn_stats(st[0:1, which, :], rows))
            then(nc.vector.bn_aggr(mv[0:1, which, :], st[0:1, which, :]))
            nc.vector.tensor_scalar(ve[0:1, which:which + 1], mv[0:1, which, 1:2], EPS, None, ALU.add)\
                .then_inc(s["var0_done"], 1)
            dve.wait_ge(s["rstd0_done"], which + 1)
            op = nc.vector.tensor_scalar(dst, rows, mv[0:1, which, 0:1], rs[0:1, which:which + 1],
                                         ALU.subtract, ALU.mult)
            if tells:
                op.then_inc(tells, 1)
            else:
                then(op)

        then(nc.vector.memset(b["s0"][0:WIN, 0, :], NEG))
        then(nc.vector.memset(b["s0"][WIN:P, NT, :], NEG))
        then(nc.vector.memset(one_row[:, :], 1.0))
        nc.vector.tensor_reduce(out=tile_max[:, :], in_=b["s0"][:, :, :].rearrange("p t h -> p h t"), axis=AX.X,
                                op=ALU.max).then_inc(s["max_done"], 1)
        dve.wait_ge(s["all_max_done"], 1)
        nc.vector.tensor_tensor(b["s0"][:, :, :], b["s0"][:, :, :],
                                all_max[:, :].rearrange("p (a h) -> p a h", a=1).broadcast_to([P, NT + 1, H]),
                                ALU.subtract).then_inc(s["less_done"], 1)
        dve.wait_ge(s["pv0_done"], 1)
        then(nc.vector.tensor_tensor(own_head[:, :, :], b["psB"][0][0:H, 0:H * DV].rearrange("p (h d) -> p h d", h=H),
                                     b["ident"][0:H, 0:H].rearrange("p (h a) -> p h a", a=1).broadcast_to([H, H, DV]),
                                     ALU.mult))
        then(nc.vector.tensor_reduce(out=od[:, :], in_=own_head[:, :, :].rearrange("p h d -> p d h"), axis=AX.X, op=ALU.add))
        then(nc.vector.reciprocal(rd[:, :], od[:, DH:DV]))
        nc.vector.tensor_scalar(diag[:, :].rearrange("p (h d) -> p h d", h=H), own_head[:, :, 0:DH], rd[:, 0:1], None,
                                ALU.mult).then_inc(s["diag_done"], 1)
        dve.wait_ge(s["col_done"], 1)
        nc.vector.tensor_copy(col[:, 0, :], b["psX"][:, 0:DC]).then_inc(s["col_copied"], 1)
        dve.wait_ge(s["pv0_done"], 2)
        then(nc.vector.tensor_tensor(row[0:1, 0, :], b["psY"][0:1, 0:D], b["bo_all"][0:1, :], ALU.add))
        norm(0, row[0:1, 1, :], row[0:1, 0, :])
        dve.wait_ge(s["xrow_in"], 16)
        nc.vector.tensor_tensor(row[0:1, 2, :], row[0:1, 1, :], xrow[:, :], ALU.add).then_inc(s["row_done"], 1)
        dve.wait_ge(s["row_done"], 1)
        norm(1, row[0:1, 3, :], row[0:1, 2, :], s["row_done"])
        dve.wait_ge(s["col_done"], 2)
        nc.vector.tensor_copy(col[:, 1, :], b["psX"][:, 0:DC]).then_inc(s["col_copied"], 1)
        dve.wait_ge(s["pv0_done"], 3)
        then(nc.vector.tensor_tensor(row[0:1, 0, :], b["psT"][0:1, 0:D], b["bf_all"][0:1, :], ALU.add))
        norm(2, row[0:1, 4, :], row[0:1, 0, :])
        nc.vector.tensor_tensor(row[0:1, 5, :], row[0:1, 4, :], row[0:1, 2, :], ALU.add).then_inc(s["row_done"], 1)


_INS = ["L0_attn_x", "L0_attn_Wq", "L0_attn_bq", "L0_attn_Wk", "L0_attn_bk", "L0_attn_Wv", "L0_attn_bv",
        "L0_attn_Wo", "L0_attn_bo", "L0_ffn_w_freq_real", "L0_ffn_w_freq_imag", "L0_ffn_bias"]


def constants():
    n = np.arange(D)
    angle = 2.0 * np.pi * (np.outer(n, n) % D) / D
    r, c = (np.arange(P) % WIN)[:, None], np.arange(AW)[None, :]
    mask = np.where((c < r) | (c > r + 2 * WIN), NEG, 0.0)
    krows = np.zeros((3, SP_))
    krows[0, :WIN + 1] = NEG
    krows[0, WIN + S:] = NEG
    krows[1:] = 1.0
    return {"ident": np.eye(P, dtype=np.float32), "mask": mask.astype(np.float32),
            "krows": krows.astype(np.float32),
            "cos": np.cos(angle).astype(np.float32), "sin": np.sin(angle).astype(np.float32)}


def kernel(**inputs):
    import concourse.bacc as _bacc
    from concourse.bass_utils import run_bass_kernel_spmd as _run

    nc = _bacc.Bacc("TRN2", target_bir_lowering=False, num_devices=1)
    arrays, args = {}, []
    for name, a in [(n, inputs[n]) for n in _INS] + list(constants().items()):
        a = np.ascontiguousarray(a)
        arrays[f"in_{name}"] = a
        args.append(nc.dram_tensor(f"in_{name}", a.shape, mybir.dt.from_np(a.dtype), kind="ExternalInput").ap())
    out = nc.dram_tensor("out", (1, S, D), F32, kind="ExternalOutput").ap()
    build(nc, *args, out)
    r = _run(nc, [arrays], core_ids=[0])
    return r.results[0]["out"]
```

```python
from contextlib import ExitStack

import numpy as np

import concourse.bass as bass
from concourse import mybir

F32 = mybir.dt.float32
BF16 = mybir.dt.bfloat16
ALU = mybir.AluOpType
ACT = mybir.ActivationFunctionType
AX = mybir.AxisListType

S, D, H = 4096, 256, 16
DH = D // H
DV = DH + 1
WIN = 64
P = 128
EPS = 1e-5
NEG = -1e30
SCALE = DH ** -0.5
DC = D // P
NT = S // P
SP_ = S + 2 * WIN
C1 = 512
N1 = S // C1
B1 = C1 // P
C2 = 256
NF = S // C2
BF = C2 // P
KF = C2 + 2 * WIN
RING = 4
BODY = RING * BF
LEAD = 4
AW = 3 * WIN
NG = 4
QPARTS = (0, 0, 0, 1, 1, 2)
KPARTS = (0, 1, 2, 0, 1, 0)
R_PROD = 16 * len(QPARTS)
R_PAD = R_PROD
R_MAX = R_PROD + 1
K_MAXPASS = R_PAD + 1
K_PROB = R_MAX + 2

S_PV = 2
S_OV = NG + 1
S_T1 = 6
S_DIV = 7
S_T2 = 8
S_WO = 9
S_ST1 = 10
S_RT1 = 11
S_Z1 = 12
S_X1 = 13
S_ST2 = 14
S_RT2 = 15
S_H2 = 17
S_T3 = 18
S_FF = 19
S_ST3 = 20
S_RT3 = 22
S_Z3 = 25
S_RES = 26
S_OUT = 27


def build(nc, x, Wq, bq, Wk, bk, Wv, bv, Wo, bo, w_re, w_im, ff_bias, ident_d, mask_d, krows_d,
          cos_d, sin_d, out):
    q_parts = nc.dram_tensor("q_parts", [3, D, S], BF16, kind="Internal").ap()
    k_parts = nc.dram_tensor("k_parts", [3, D, SP_], BF16, kind="Internal").ap()
    krows_b = nc.dram_tensor("krows_b", [3, SP_], BF16, kind="Internal").ap()
    v_rows = nc.dram_tensor("v_rows", [SP_, H * DV], F32, kind="Internal").ap()

    ctx = ExitStack()
    with ctx:
        def sb(name, shape, dt=F32):
            return ctx.enter_context(nc.sbuf_tensor(name, shape, dt))

        def sem(name):
            return ctx.enter_context(nc.semaphore(name))

        ident = sb("ident", [P, P])
        ident_b = sb("ident_b", [P, P], BF16)
        mask_f = sb("mask_f", [P, 4 * WIN])
        mask_b = sb("mask_b", [P, 4 * WIN], BF16)
        wq, wk, wv, wo = (sb(n, [P, DC, D]) for n in ("wq", "wk", "wv", "wo"))
        mff = sb("mff", [P, DC, D])
        bqk = sb("bqk", [P, 2, DC])
        bv_all, bo_all, bf_all = (sb(n, [P, D]) for n in ("bv_all", "bo_all", "bf_all"))
        minus_half = sb("minus_half", [P, B1])
        psA = ctx.enter_context(nc.psum_tensor("psA", [P, 2, 512], F32))
        psB = [ctx.enter_context(nc.psum_tensor(f"psB{i}", [P, 512], F32)) for i in range(2)]
        psV = ctx.enter_context(nc.psum_tensor("psV", [P, 512], F32))
        psT = ctx.enter_context(nc.psum_tensor("psT", [P, 512], F32))
        psX = ctx.enter_context(nc.psum_tensor("psX", [P, 512], F32))
        psY = ctx.enter_context(nc.psum_tensor("psY", [P, 512], F32))

        s0 = sb("s0", [P, NT + 1, H])
        b = dict(locals())
        stage0(nc, b)
        with ExitStack() as own:
            stage1(nc, own, b)
        with ExitStack() as own:
            stage2(nc, own, b)
        with ExitStack() as own:
            stage3(nc, own, b)


def stage0(nc, b):
    with ExitStack() as own:
        def sb(name, shape):
            return own.enter_context(nc.sbuf_tensor(name, shape, F32))

        wre, wim, cosm, sinm = (sb(n, [P, DC, D]) for n in ("wre", "wim", "cosm", "sinm"))
        nsin = sb("nsin", [P, DC, D])
        grT, giT = sb("grT", [P, DC, D]), sb("giT", [P, DC, D])
        zb = own.enter_context(nc.sbuf_tensor("zb", [P, 3 * DC * WIN], BF16))
        zf = sb("zf", [WIN, H * DV])
        krows = sb("krows", [3, SP_])
        krows_h = own.enter_context(nc.sbuf_tensor("krows_h", [3, SP_], BF16))
        weights_in, consts_in = (own.enter_context(nc.semaphore(n)) for n in ("weights_in", "consts_in"))
        pads_out, zeros_set, const_set, nsin_set, g_done, g_copied, m_done, m_set = (
            own.enter_context(nc.semaphore(n)) for n in (
                "pads_out", "zeros_set", "const_set", "nsin_set", "g_done", "g_copied", "m_done", "m_set"))
        block = own.enter_context(nc.Block())
        rows = "(c p) n -> p c n"

        @block.sync
        def _(sp):
            for dst, src in ((wre, b["w_re"]), (wim, b["w_im"]), (cosm, b["cos_d"]), (sinm, b["sin_d"])):
                sp.dma_start(dst[:, :, :], src.rearrange(rows, p=P)).then_inc(weights_in, 16)
            sp.dma_start(b["ident"][:, :], b["ident_d"]).then_inc(consts_in, 16)
            sp.dma_start(krows[:, :], b["krows_d"]).then_inc(consts_in, 16)
            for i in range(2):
                sp.dma_start(b["mask_f"][:, i * 2 * WIN:(i + 1) * 2 * WIN], b["mask_d"]).then_inc(consts_in, 16)
            for i, src in enumerate((b["bq"], b["bk"])):
                for c in range(DC):
                    sp.dma_start(b["bqk"][:, i, c:c + 1], src[c * P:(c + 1) * P].rearrange("(p a) -> p a", a=1))\
                        .then_inc(consts_in, 16)
            for dst, src in ((b["wq"], b["Wq"]), (b["wk"], b["Wk"]), (b["wv"], b["Wv"]), (b["wo"], b["Wo"])):
                sp.dma_start(dst[:, :, :], src.rearrange(rows, p=P)).then_inc(consts_in, 16)
            for dst, src in ((b["bv_all"], b["bv"]), (b["bo_all"], b["bo"]), (b["bf_all"], b["ff_bias"])):
                sp.dma_start(dst[:, :], src.rearrange("(a n) -> a n", a=1).broadcast_to([P, D])).then_inc(consts_in, 16)
            sp.wait_ge(zeros_set, 2)
            for at in (0, WIN + S):
                sp.dma_start(b["k_parts"][:, :, at:at + WIN].rearrange("t (c p) n -> p (t c) n", p=P),
                             zb[:, :].rearrange("p (t n) -> p t n", n=WIN)).then_inc(pads_out, 16)
                sp.dma_start(b["v_rows"][at:at + WIN, :], zf[:, :]).then_inc(pads_out, 16)
            sp.wait_ge(nsin_set, 5)
            sp.dma_start(b["krows_b"], krows_h[:, :]).then_inc(pads_out, 16)
            sp.wait_ge(pads_out, 16 * 5)
            sp.wait_ge(consts_in, 16 * 15)

        @block.gpsimd
        def _(pool):
            nc.gpsimd.memset(b["minus_half"][:, :], -0.5).then_inc(const_set, 1)
            pool.wait_ge(const_set, 1)

        @block.vector
        def _(dve):
            nc.vector.memset(zb[:, :], 0.0).then_inc(zeros_set, 1)
            nc.vector.memset(zf[:, :], 0.0).then_inc(zeros_set, 1)
            dve.wait_ge(weights_in, 16 * 4)
            nc.vector.tensor_scalar(nsin[:, :, :], sinm[:, :, :], -1.0, None, ALU.mult).then_inc(nsin_set, 1)
            dve.wait_ge(consts_in, 16 * 15)
            nc.vector.tensor_copy(b["ident_b"][:, :], b["ident"][:, :]).then_inc(nsin_set, 1)
            nc.vector.tensor_copy(b["mask_b"][:, :], b["mask_f"][:, :]).then_inc(nsin_set, 1)
            nc.vector.tensor_scalar(b["bqk"][:, 0, :], b["bqk"][:, 0, :], SCALE, None, ALU.mult).then_inc(nsin_set, 1)
            nc.vector.tensor_copy(krows_h[:, :], krows[:, :]).then_inc(nsin_set, 1)
            for i, (ps, dst) in enumerate(((b["psB"][0], grT), (b["psB"][1], giT))):
                dve.wait_ge(g_done, i + 1)
                nc.vector.tensor_copy(dst[:, :, :].rearrange("p c n -> p (c n)"), ps[:, :]).then_inc(g_copied, 1)
            dve.wait_ge(m_done, 1)
            nc.vector.tensor_scalar(b["mff"][:, :, :].rearrange("p c n -> p (c n)"), b["psT"][:, :], 1.0 / D, None,
                                    ALU.mult).then_inc(m_set, 1)
            dve.wait_ge(nsin_set, 5)
            dve.wait_ge(m_set, 1)

        @block.tensor
        def _(pe):
            pe.wait_ge(weights_in, 16 * 4)
            pe.wait_ge(nsin_set, 1)
            for ps, terms in ((b["psB"][0], ((wre, cosm), (wim, sinm))), (b["psB"][1], ((wim, cosm), (wre, nsin)))):
                for o in range(DC):
                    for i, (w, f) in enumerate(terms):
                        for c in range(DC):
                            mm = nc.tensor.matmul(ps[:, o * D:(o + 1) * D], w[:, c, o * P:(o + 1) * P], f[:, c, :],
                                                  start=(i + c == 0), stop=(i == 1 and c == DC - 1))
                mm.then_inc(g_done, 1)
            pe.wait_ge(g_copied, 2)
            for o in range(DC):
                for i, (g, f) in enumerate(((grT, cosm), (giT, nsin))):
                    for c in range(DC):
                        mm = nc.tensor.matmul(b["psT"][:, o * D:(o + 1) * D], g[:, c, o * P:(o + 1) * P], f[:, c, :],
                                              start=(i + c == 0), stop=(i == 1 and c == DC - 1))
            mm.then_inc(m_done, 1)


def stage1(nc, own, b):
    def sb(name, shape, dt=F32):
        return own.enter_context(nc.sbuf_tensor(name, shape, dt))

    xc = sb("xc", [P, 2, B1, D])
    hc = sb("hc", [P, 2, B1, D])
    hT = sb("hT", [P, 2, DC, C1])
    full = sb("full", [P, 2, DC, C1])
    left = sb("left", [P, 2, 2, DC, C1])
    part = sb("part", [P, 2, 2, 3, DC, C1], BF16)
    vrow = sb("vrow", [P, 2, B1, H, DV])
    bv2 = sb("bv2", [P, 2, D])
    st1 = sb("st1", [P, B1, 6])
    mv1 = sb("mv1", [P, B1, 2])
    ve1 = sb("ve1", [P, B1])
    rs1 = sb("rs1", [P, B1])
    CREDIT = {"h_done": 2, "turned": 2, "hT_copied": 1, "part1_done": 2, "left_done": 2,
              "part3_done": 4, "v_done": 4, "v_copied": 2}
    s = {n: own.enter_context(nc.semaphore(n)) for n in (
        "stats_done", "aggr_done", "var_done", "rstd_done", "h_done", "turned", "hT_copied", "qk_done",
        "v_done", "part1_done", "left_done", "part2_done", "part3_done", "v_copied", "ones_set", "passed")}
    x_in = [own.enter_context(nc.semaphore(f"x_in{i}")) for i in range(2)]
    qk_out = [own.enter_context(nc.semaphore(f"qk_out{i}")) for i in range(4)]
    v_out = [own.enter_context(nc.semaphore(f"v_out{i}")) for i in range(2)]
    psQK = [[b["psB"][0], b["psB"][1]], [b["psX"], b["psY"]]]
    psVV = [b["psV"], b["psT"]]
    block = own.enter_context(nc.Block())
    PAIRS = N1 // 2

    def after(eng, name, n):
        eng.wait_ge(s[name], n + CREDIT.get(name, 0))

    def apart(eng):
        eng.sem_inc(s["passed"], 1)

    def chunks(eng, body):
        with eng.Fori(0, PAIRS - 1) as i:
            for par in range(2):
                body(i * 2 + par, par, i, False)
        for par in range(2):
            body(N1 - 2 + par, par, PAIRS - 1, True)

    @block.sync
    def _(sp):
        for w in range(4):
            sp.sem_inc(qk_out[w], 48)
        for w in range(2):
            sp.sem_inc(v_out[w], 16)
        for name, n in CREDIT.items():
            sp.sem_inc(s[name], n)

        def load(c, par):
            after(sp, "h_done", c - 1)
            sp.dma_start(xc[:, par, :, :],
                         b["x"][0, bass.ds(c * C1, C1), :].rearrange("(j p) d -> p j d", p=P)).then_inc(x_in[par], 16)

        def body(c, par, use, last):
            if not last:
                load(c + 2, par)
            for w, (dst, pad) in enumerate(((b["q_parts"], 0), (b["k_parts"], WIN))):
                after(sp, "part3_done", c * 2 + w + 1)
                for t in range(3):
                    sp.dma_start(dst[t, :, bass.ds(c * C1 + pad, C1)].rearrange("(o p) n -> p o n", p=P),
                                 part[:, par, w, t, :, :]).then_inc(qk_out[2 * par + w], 16)
            after(sp, "v_copied", c * 2 + 2)
            sp.dma_start(b["v_rows"][bass.ds(c * C1 + WIN, C1), :].rearrange("(j p) n -> p j n", p=P),
                         vrow[:, par, :, :, :].rearrange("p j h d -> p j (h d)")).then_inc(v_out[par], 16)

        load(0, 0)
        load(1, 1)
        chunks(sp, body)
        for w in range(2):
            sp.wait_ge(v_out[w], 16 * (PAIRS + 1))
        for w in range(4):
            sp.wait_ge(qk_out[w], 48 * (PAIRS + 1))

    @block.vector
    def _(dve):
        ones = vrow[:, :, :, :, DH:DV].rearrange("p a j h d -> p (a j h) d")
        nc.vector.memset(ones, 1.0).then_inc(s["ones_set"], 1)
        for j in range(2):
            nc.vector.tensor_copy(bv2[:, j, :], b["bv_all"][:, :]).then_inc(s["ones_set"], 1)
        dve.wait_ge(s["ones_set"], 3)

        def norm(c, par, use):
            dve.wait_ge(x_in[par], use * 16 + 16)
            for j in range(B1):
                nc.vector.bn_stats(st1[:, j, :], xc[:, par, j, :]).then_inc(s["stats_done"], 1)
            for j in range(B1):
                after(dve, "stats_done", c * B1 + j + 1)
                apart(dve)
                nc.vector.bn_aggr(mv1[:, j, :], st1[:, j, :]).then_inc(s["aggr_done"], 1)
            after(dve, "aggr_done", c * B1 + B1)
            nc.vector.tensor_scalar(ve1[:, :], mv1[:, :, 1], EPS, None, ALU.add).then_inc(s["var_done"], 1)
            after(dve, "rstd_done", c + 1)
            after(dve, "turned", c - 1)
            for j in range(B1):
                op = nc.vector.tensor_scalar(hc[:, par, j, :], xc[:, par, j, :], mv1[:, j, 0:1], rs1[:, j:j + 1],
                                             ALU.subtract, ALU.mult)
            op.then_inc(s["h_done"], 1)
            after(dve, "h_done", c + 1)

        def body(c, par, use, last):
            if not (last and par == 1):
                norm(c + 1, 1 - par, use + par)
            for w in range(2):
                after(dve, "part1_done", c * 2 + w + 1)
                after(dve, "part3_done", c * 2 + w - 3)
                nc.vector.tensor_tensor(left[:, par, w], full[:, w], part[:, par, w, 0], ALU.subtract)\
                    .then_inc(s["left_done"], 1)
                after(dve, "left_done", c * 2 + w + 1)
                nc.vector.tensor_copy(part[:, par, w, 1], left[:, par, w]).then_inc(s["part2_done"], 1)
            dve.wait_ge(v_out[par], 16 * use + 16)
            for half in range(2):
                after(dve, "v_done", c * 2 + half + 1)
                nc.vector.tensor_tensor(
                    vrow[:, par, 2 * half:2 * half + 2, :, 0:DH].rearrange("p j h d -> p (j h) d"),
                    psVV[half][:, :].rearrange("p (g d) -> p g d", d=DH),
                    bv2[:, :, :].rearrange("p j (h d) -> p (j h) d", d=DH), ALU.add).then_inc(s["v_copied"], 1)

        norm(0, 0, 0)
        chunks(dve, body)

    @block.gpsimd
    def _(pool):
        def rstd(c):
            after(pool, "var_done", c + 1)
            nc.gpsimd.tensor_tensor(rs1[:, :], ve1[:, :], b["minus_half"][:, :], ALU.pow).then_inc(s["rstd_done"], 1)

        def body(c, par, use, last):
            if not (last and par == 1):
                rstd(c + 1)
            for w in range(2):
                after(pool, "part2_done", c * 2 + w + 1)
                nc.gpsimd.tensor_tensor(part[:, par, w, 2], left[:, par, w], part[:, par, w, 1], ALU.subtract)\
                    .then_inc(s["part3_done"], 1)

        rstd(0)
        chunks(pool, body)

    @block.scalar
    def _(act):
        def hT_copy(c, par):
            after(act, "turned", c + 1)
            after(act, "v_done", c * 2 - 2)
            nc.scalar.copy(hT[:, par, :, :], b["psA"][:, :, :]).then_inc(s["hT_copied"], 1)

        def body(c, par, use, last):
            for w in range(2):
                act.wait_ge(s["qk_done"], c * 2 + w + 1)
                after(act, "left_done", c * 2 + w - 1)
                act.wait_ge(qk_out[2 * par + w], 48 * use + 48)
                for o in range(DC):
                    for dst in (full[:, w, o, :], part[:, par, w, 0, o, :]):
                        op = nc.scalar.activation(dst, psQK[w][o][:, :], ACT.Identity, bias=b["bqk"][:, w, o:o + 1],
                                                  scale=(SCALE, 1.0)[w])
                op.then_inc(s["part1_done"], 1)
            if not (last and par == 1):
                hT_copy(c + 1, 1 - par)

        hT_copy(0, 0)
        chunks(act, body)

    @block.tensor
    def _(pe):
        def turn(c, par):
            after(pe, "h_done", c + 1)
            after(pe, "hT_copied", c)
            for j in range(B1):
                for d in range(DC):
                    op = nc.tensor.transpose(b["psA"][:, d, j * P:(j + 1) * P], hc[:, par, j, d * P:(d + 1) * P],
                                             b["ident"][:, :])
            op.then_inc(s["turned"], 1)

        def body(c, par, use, last):
            after(pe, "hT_copied", c + 1)
            for w, weight in enumerate((b["wq"], b["wk"])):
                after(pe, "part1_done", c * 2 + w - 1)
                for o in range(DC):
                    for d in range(DC):
                        op = nc.tensor.matmul(psQK[w][o][:, :], weight[:, d, o * P:(o + 1) * P], hT[:, par, d, :],
                                              start=(d == 0), stop=(d == DC - 1))
                op.then_inc(s["qk_done"], 1)
            if not (last and par == 1):
                turn(c + 1, 1 - par)
            for half in range(2):
                after(pe, "v_copied", c * 2 + half - 1)
                for j in range(2):
                    t = half * 2 + j
                    for d in range(DC):
                        op = nc.tensor.matmul(psVV[half][:, j * D:(j + 1) * D], hT[:, par, d, t * P:(t + 1) * P],
                                              b["wv"][:, d, :], start=(d == 0), stop=(d == DC - 1))
                op.then_inc(s["v_done"], 1)

        turn(0, 0)
        chunks(pe, body)


def stage2(nc, own, b):
    def sb(name, shape, dt=F32):
        return own.enter_context(nc.sbuf_tensor(name, shape, dt))

    q_st = sb("q_st", [P, RING, H, C2], BF16)
    k_st = sb("k_st", [P, RING, H, KF], BF16)
    v_st = sb("v_st", [P, RING, BF + 1, H, DV])
    k0 = sb("k0", [P, H], BF16)
    q0 = sb("q0", [P, H], BF16)
    v0_all = sb("v0_all", [P, H, DV])
    nmax = sb("nmax", [P, 2, BF, H])
    gsc = sb("gsc", [P, 2, BF, H])
    ngsc = sb("ngsc", [P, BF, H])
    nshift = sb("nshift", [P, BF, H])
    hilo = sb("hilo", [P, 2, BF, 2, H], BF16)
    shift = sb("shift", [P, BF, H])
    earg = sb("earg", [P, 2, BF, H])
    eglob = sb("eglob", [P, RING, BF, H])
    shiftT = sb("shiftT", [2 * H, 2, C2], BF16)
    prob = sb("prob", [P, NG, 4, 2, P])
    gpart = sb("gpart", [P, 2, H, DV])
    oslot = sb("oslot", [P, NG, P])
    osum = sb("osum", [P, 2, H, DV])
    rden = sb("rden", [P, 2, H])
    on = sb("on", [P, 2, D])
    oT = sb("oT", [P, DC, P])
    att = sb("att", [P, 2, D])
    z1 = sb("z1", [P, 2, D])
    xin = sb("xin", [P, 4, D])
    x1 = sb("x1", [P, 4, D])
    h2 = sb("h2", [P, 2, D])
    h2T = sb("h2T", [P, DC, P])
    yff = sb("yff", [P, 2, D])
    z3 = sb("z3", [P, 2, D])
    res = sb("res", [P, 2, D])
    st = sb("st", [P, 3, 2, 6])
    mv = sb("mv", [P, 3, 2, 2])
    ve = sb("ve", [P, 3, 2])
    rs = sb("rs", [P, 3, 2])

    CREDIT = {"a_read": 2, "exp_done": 2, "pv_done": 4, "ov_done": 1, "t1_done": 1, "osum_done": 2,
              "e2_done": 1, "e3_done": 3, "wo_done": 1, "ff_done": 1, "att_read": 1, "ff_read": 3,
              "eg_done": 2, "gp_done": 8, ("z_done", 0): 2, ("z_done", 1): 2, ("z_done", 2): 2}
    s = {n: own.enter_context(nc.semaphore(n)) for n in (
        "a_done",
        "a_read",
        "shift_step",
        "shT_done",
        "eg_done",
        "b_done",
        "exp_done",
        "sel_done",
        "pv_done",
        "ov_done",
        "t1_done",
        "gp_done",
        "osum_done",
        "rden_done", "on_done",
        "t2_done",
        "e2_done",
        "wo_done",
        "att_read",
        "x1_done",
        "t3_done",
        "e3_done",
        "ff_done",
        "ff_read",
        "res_done",
        "first_rows", "cleared", "passed")}
    for n in ("stat_done", "aggr_done", "var_done", "rstd_done", "z_done"):
        for which in range(3):
            s[n, which] = own.enter_context(nc.semaphore(f"{n}{which}"))
    frame_in = [own.enter_context(nc.semaphore(f"frame_in{i}")) for i in range(RING)]
    v_in = [own.enter_context(nc.semaphore(f"v_in{i}")) for i in range(RING)]
    x_in = [own.enter_context(nc.semaphore(f"xblock_in{i}")) for i in range(4)]
    shift_in = [own.enter_context(nc.semaphore(f"shift_in{i}")) for i in range(2)]
    out_st = [own.enter_context(nc.semaphore(f"out_st{i}")) for i in range(2)]
    v0_in = own.enter_context(nc.semaphore("v0_in"))
    FRAME_DMAS = len(QPARTS) + len(KPARTS) + 1
    block = own.enter_context(nc.Block())
    BODIES = NT // BODY
    SLOTS = NG * BODY

    def after(eng, name, n):
        eng.wait_ge(s[name], n + CREDIT.get(name, 0))

    def apart(eng):
        eng.sem_inc(s["passed"], 1)

    def bodies(eng, step):
        for slot in range(SLOTS):
            step(slot, 0, True, False)
        with eng.Fori(1, BODIES - 1) as i:
            for slot in range(SLOTS):
                step(slot, i, False, False)
        for slot in range(SLOTS + S_OUT + 1 - NG):
            step(slot, BODIES - 1, False, True)

    def main(slot):
        return divmod(slot, NG) if slot < SLOTS else None

    def at(slot, offset, first):
        k, rest = divmod(slot - offset, NG)
        return k if rest == 0 and k < BODY and (k >= 0 or not first) else None

    def before(k, mine, other, last):
        n = (NG * k + mine - other) // NG + 1
        return min(n, BODY) if last else n

    def ahead(k, last):
        return not last or k + LEAD < BODY

    @block.sync
    def _(sp):
        for name, n in CREDIT.items():
            sp.sem_inc(s[name], n)
        for i in range(2):
            sp.sem_inc(shift_in[i], 32)
            sp.sem_inc(out_st[i], 16)

        def load_frame(f, r):
            for i, t in enumerate(QPARTS):
                sp.dma_start(q_st[16 * i:16 * i + 16, r, :, :],
                             b["q_parts"][t, :, bass.ds(f * C2, C2)].rearrange("(h d) n -> d h n", d=DH))\
                    .then_inc(frame_in[r], 16)
            for i, t in enumerate(KPARTS):
                sp.dma_start(k_st[16 * i:16 * i + 16, r, :, :],
                             b["k_parts"][t, :, bass.ds(f * C2, KF)].rearrange("(h d) n -> d h n", d=DH))\
                    .then_inc(frame_in[r], 16)
            sp.dma_start(k_st[R_PAD:R_MAX + 2, r, :, :],
                         b["krows_b"][:, bass.ds(f * C2, KF)].rearrange("r (a n) -> r a n", a=1)
                         .broadcast_to([3, H, KF])).then_inc(frame_in[r], 16)

        def load_v(f, r):
            sp.dma_start(v_st[:, r, :, :, :].rearrange("p t h d -> p t (h d)"),
                         b["v_rows"][bass.ds(f * C2, (BF + 1) * P), :].rearrange("(t p) n -> p t n", p=P))\
                .then_inc(v_in[r], 16)

        def load_x(n, k):
            sp.dma_start(xin[:, k % 4, :], b["x"][0, bass.ds(n * P, P), :]).then_inc(x_in[k % 4], 16)

        def place_shifts(i, kf):
            after(sp, "shT_done", i * RING + kf + 1)
            for part in range(2):
                sp.dma_start(q_st[R_MAX + part:R_MAX + part + 1, kf % RING, :, :],
                             shiftT[part * H:part * H + H, kf % 2, :]).then_inc(shift_in[kf % 2], 16)

        def step(slot, i, first, last):
            base = i * BODY
            if main(slot):
                k, g = main(slot)
                if k % 2 == 0 and g == 2:
                    if ahead(k, last) or k == LEAD:
                        place_shifts(i, (k + LEAD) // BF - 1)
            k = at(slot, S_OV + 1, first)
            if k is not None and k % BF == BF - 1 and (not last or k < 0):
                after(sp, "b_done", 8 * (base + k) + 8)
                load_frame((i + 1) * RING + k // BF, k // BF % RING)
                after(sp, "pv_done", 4 * (base + k) + 4)
                load_v((i + 1) * RING + k // BF, k // BF % RING)
            k = at(slot, S_X1 + 1, first)
            if k is not None and (not last or k + 4 < BODY):
                after(sp, "x1_done", base + k + 1)
                load_x(base + k + 4, k)
            k = at(slot, S_OUT, first)
            if k is not None:
                after(sp, "res_done", base + k + 1)
                sp.dma_start(b["out"][0, bass.ds((base + k) * P, P), :], res[:, k % 2, :]).then_inc(out_st[k % 2], 16)

        sp.wait_ge(s["cleared"], 1)
        for f in range(RING):
            load_frame(f, f)
            if f == 0:
                sp.dma_start(v0_all[:, :, :].rearrange("p h d -> p (h d)"),
                             b["v_rows"][WIN:WIN + 1, :].broadcast_to([P, H * DV])).then_inc(v0_in, 16)
        for f in range(RING):
            load_v(f, f)
            load_x(f, f)
        place_shifts(0, 0)
        bodies(sp, step)
        for i in range(2):
            sp.wait_ge(out_st[i], 16 * (NT // 2 + 1))

    @block.tensor
    def _(pe):
        def maxima(i, km, u):
            m, use, bank = i * BODY + km, i + km // BODY, u % 2
            r, j = km // BF % RING, km % BF
            after(pe, "a_read", 8 * m + u - 1)
            if u == 0:
                pe.wait_ge(frame_in[r], 16 * FRAME_DMAS * (use + 1))
                if km == 0:
                    pe.wait_ge(s["first_rows"], 2)
            for hh in range(2):
                h = 2 * u + hh
                for t in range(2):
                    c = j * P + t * WIN
                    op = nc.tensor.matmul(b["psA"][t * WIN:t * WIN + WIN, bank, hh * AW:hh * AW + AW],
                                          q_st[0:K_MAXPASS, r, h, c:c + WIN], k_st[0:K_MAXPASS, r, h, c:c + AW],
                                          start=(hh == 0), stop=False, skip_group_check=True)
            edges = b["psA"][:, bank, 0:2 * AW].rearrange("p (h e n) -> p h e n", h=2, n=WIN)[:, :, 0:3:2, :]
            op = nc.tensor.matmul(edges, b["ident_b"][:, :], b["mask_b"][:, :], start=False, stop=True,
                                  skip_group_check=True)
            if u == 0:
                for h in range(H):
                    nc.tensor.matmul(b["psA"][:, 0, 2 * AW + h:2 * AW + h + 1], q_st[0:R_PROD, r, h, j * P:j * P + P],
                                     k0[0:R_PROD, h:h + 1], start=True, stop=True)
                op = query0(r, j)
            if u == 5 and km % BF == 0 and km > 0:
                op = turn_shifts(i, km)
            op.then_inc(s["a_done"], 1)

        def query0(r, j):
            for h in range(H):
                op = nc.tensor.matmul(b["psA"][:, 0, 2 * AW + H + h:2 * AW + H + h + 1],
                                      k_st[0:R_PROD, r, h, j * P:j * P + P], q0[0:R_PROD, h:h + 1],
                                      start=True, stop=True)
            return op

        def turn_shifts(i, km):
            kf = km // BF - 1
            after(pe, "shift_step", 6 * (i * RING + kf) + 4)
            for j in range(BF):
                op = nc.tensor.transpose(
                    b["psA"][0:2 * H, 1, 2 * AW + j * WIN:2 * AW + (j + 1) * WIN].bitcast(BF16),
                    hilo[:, kf % 2, j, :, :].rearrange("p a h -> p (a h)"), b["ident_b"][:, :])
            return op

        def scores(n, k, u):
            r, j = k // BF % RING, k % BF
            after(pe, "exp_done", 8 * n + u - 1)
            for hh in range(2):
                for t in range(2):
                    c = (hh * 2 + t) * P
                    op = nc.tensor.matmul(b["psB"][u % 2][:, c:c + P],
                                          k_st[0:K_PROB, r, 2 * u + hh, (j + t) * P:(j + t + 1) * P],
                                          q_st[0:K_PROB, r, 2 * u + hh, j * P:j * P + P], start=True, stop=True)
            op.then_inc(s["b_done"], 1)

        def values(n, k, g):
            r, j = k // BF % RING, k % BF
            after(pe, "sel_done", 8 * n + 2 * g + 2)
            if g == 0:
                after(pe, "ov_done", n)
            for t in range(2):
                for hq in range(4):
                    op = nc.tensor.matmul(b["psV"][32 * hq:32 * hq + DV, g * P:g * P + P], v_st[:, r, j + t, 4 * g + hq, :],
                                          prob[:, g, hq, t, :], start=(t == 0), stop=(t == 1), skip_group_check=True)
            op.then_inc(s["pv_done"], 1)

        def step(slot, i, first, last):
            base = i * BODY
            if main(slot):
                k, g = main(slot)
                n = base + k
                if ahead(k, last):
                    maxima(i, k + LEAD, 2 * g)
                elif k == LEAD and g == 0:
                    after(pe, "a_read", 8 * NT)
                    query0(RING - 1, BF).then_inc(s["a_done"], 1)
                elif k == LEAD and g == 2:
                    after(pe, "a_read", 8 * NT + 1)
                    turn_shifts(i, k + LEAD).then_inc(s["a_done"], 1)
                if g == 0 and k % BF == 0:
                    pe.wait_ge(shift_in[k // BF % 2], (i * (RING // 2) + k // BF // 2 + 2) * 32)
                    pe.wait_ge(v_in[k // BF], 16 * (i + 1))
                scores(n, k, 2 * g)
                if ahead(k, last):
                    maxima(i, k + LEAD, 2 * g + 1)
                scores(n, k, 2 * g + 1)
            if slot - S_PV < SLOTS and not (first and slot < S_PV):
                k, g = divmod(slot - S_PV, NG)
                values(base + k, k, g)
            if (k := at(slot, S_T3, first)) is not None:
                n = base + k
                after(pe, ("z_done", 1), n + 1)
                after(pe, "e3_done", n)
                after(pe, "e2_done", base + before(k, S_T3, S_T2, last))
                for c in range(DC):
                    op = nc.tensor.transpose(b["psX"][:, D + c * P:D + c * P + P], h2[:, k % 2, c * P:c * P + P], b["ident"][:, :])
                op.then_inc(s["t3_done"], 1)
            if (k := at(slot, S_FF, first)) is not None:
                n = base + k
                after(pe, "e3_done", n + 1)
                after(pe, "ff_read", n)
                after(pe, "att_read", base + before(k, S_FF, S_WO, last))
                for c in range(DC):
                    op = nc.tensor.matmul(b["psY"][:, D:2 * D], h2T[:, c, :], b["mff"][:, c, :], start=(c == 0), stop=(c == DC - 1))
                op.then_inc(s["ff_done"], 1)
            if (k := at(slot, S_T1, first)) is not None:
                n = base + k
                after(pe, "ov_done", n + 1)
                after(pe, "osum_done", n)
                for g in range(NG):
                    op = nc.tensor.transpose(b["psT"][:, g * P:g * P + P], oslot[:, g, :], b["ident"][:, :])
                op.then_inc(s["t1_done"], 1)
            if (k := at(slot, S_T2, first)) is not None:
                n = base + k
                after(pe, "on_done", n + 1)
                after(pe, "e2_done", n)
                after(pe, "e3_done", base + before(k, S_T2, S_T3, last))
                for c in range(DC):
                    op = nc.tensor.transpose(b["psX"][:, c * P:c * P + P], on[:, k % 2, c * P:c * P + P], b["ident"][:, :])
                op.then_inc(s["t2_done"], 1)
            if (k := at(slot, S_WO, first)) is not None:
                n = base + k
                after(pe, "e2_done", n + 1)
                after(pe, "att_read", n)
                after(pe, "ff_read", base + before(k, S_WO, S_FF, last))
                for c in range(DC):
                    op = nc.tensor.matmul(b["psY"][:, 0:D], oT[:, c, :], b["wo"][:, c, :], start=(c == 0), stop=(c == DC - 1))
                op.then_inc(s["wo_done"], 1)

        for m in range(LEAD):
            for u in range(2 * NG):
                maxima(0, m, u)
        bodies(pe, step)

    @block.vector
    def _(dve):
        def take_maxima(i, km, u):
            m, j, fp, bank = i * BODY + km, km % BF, km // BF % 2, u % 2
            after(dve, "a_done", 8 * m + u + 1)
            if u == 0:
                nc.vector.tensor_copy(gsc[:, fp, j, :], b["psA"][:, 0, 2 * AW:2 * AW + H])
                take_query0(m)
            if u == 5 and km % BF == 0 and km > 0:
                copy_shifts(i, km)
            nc.vector.tensor_reduce(out=nmax[:, fp, j, 2 * u:2 * u + 2],
                                    in_=b["psA"][:, bank, 0:2 * AW].rearrange("p (h k) -> p h k", h=2),
                                    axis=AX.X, op=ALU.max, negate=True).then_inc(s["a_read"], 1)

        def take_query0(m):
            return nc.vector.tensor_copy(b["s0"][:, bass.ds(m, 1), :].rearrange("p a h -> p (a h)"),
                                         b["psA"][:, 0, 2 * AW + H:2 * AW + 2 * H])

        def copy_shifts(i, km):
            kf = km // BF - 1
            dve.wait_ge(shift_in[kf % 2], (i * (RING // 2) + kf // 2 + 1) * 32)
            return nc.vector.tensor_copy(shiftT[:, kf % 2, :], b["psA"][0:2 * H, 1, 2 * AW:512].bitcast(BF16))\
                .then_inc(s["shT_done"], 1)

        def find_shifts(i, km):
            f, fp = i * RING + km // BF, km // BF % 2
            after(dve, "a_read", 8 * (i * BODY + km) + 8)
            nc.vector.tensor_scalar(ngsc[:, :, :], gsc[:, fp], -1.0, None, ALU.mult).then_inc(s["shift_step"], 1)
            after(dve, "shift_step", 6 * f + 1)
            nc.vector.tensor_tensor(nshift[:, :, :], nmax[:, fp], ngsc[:, :, :], ALU.min).then_inc(s["shift_step"], 1)
            after(dve, "shift_step", 6 * f + 2)
            nc.vector.tensor_copy(hilo[:, fp, :, 0, :], nshift[:, :, :]).then_inc(s["shift_step"], 1)
            after(dve, "shift_step", 6 * f + 3)
            nc.vector.tensor_tensor(hilo[:, fp, :, 1, :], nshift[:, :, :], hilo[:, fp, :, 0, :], ALU.subtract)\
                .then_inc(s["shift_step"], 1)
            after(dve, "shift_step", 6 * f + 4)
            nc.vector.tensor_tensor(shift[:, :, :], hilo[:, fp, :, 0, :], hilo[:, fp, :, 1, :], ALU.add)\
                .then_inc(s["shift_step"], 1)
            after(dve, "shift_step", 6 * f + 5)
            after(dve, "eg_done", f - 1)
            nc.vector.tensor_tensor(earg[:, fp], gsc[:, fp], shift[:, :, :], ALU.add).then_inc(s["shift_step"], 1)

        def statistics(*norms):
            for n, k, which, rows in norms:
                nc.vector.bn_stats(st[:, which, k % 2, :], rows).then_inc(s["stat_done", which], 1)
            for n, k, which, rows in norms:
                after(dve, ("stat_done", which), n + 1)
                apart(dve)
                nc.vector.bn_aggr(mv[:, which, k % 2, :], st[:, which, k % 2, :]).then_inc(s["aggr_done", which], 1)
            for n, k, which, rows in norms:
                after(dve, ("aggr_done", which), n + 1)
                nc.vector.tensor_scalar(ve[:, which, k % 2:k % 2 + 1], mv[:, which, k % 2, 1:2], EPS, None, ALU.add)\
                    .then_inc(s["var_done", which], 1)

        def normalise(n, k, which, dst, rows):
            p = k % 2
            after(dve, ("rstd_done", which), n + 1)
            nc.vector.tensor_scalar(dst, rows, mv[:, which, p, 0:1], rs[:, which, p:p + 1], ALU.subtract, ALU.mult)\
                .then_inc(s["z_done", which], 1)

        def step(slot, i, first, last):
            base = i * BODY
            if main(slot):
                k, g = main(slot)
                if ahead(k, last):
                    take_maxima(i, k + LEAD, 2 * g)
                    take_maxima(i, k + LEAD, 2 * g + 1)
                elif k == LEAD and g == 0:
                    after(dve, "a_done", 8 * NT + 1)
                    take_query0(NT).then_inc(s["a_read"], 1)
                elif k == LEAD and g == 2:
                    after(dve, "a_done", 8 * NT + 2)
                    copy_shifts(i, k + LEAD)
                if g == 0 and (k - 1 + LEAD) % BF == BF - 1 and not (first and k == 0) and (k == 0 or ahead(k - 1, last)):
                    find_shifts(i, k - 1 + LEAD)
            if (k := at(slot, S_DIV, first)) is not None:
                n, p = base + k, k % 2
                after(dve, "t1_done", n + 1)
                after(dve, "gp_done", n + 1)
                nc.vector.tensor_tensor(osum[:, p], b["psT"][:, :].rearrange("p (h d) -> p h d", h=H)[:, :, 0:DV],
                                        gpart[:, p], ALU.add).then_inc(s["osum_done"], 1)
                after(dve, "osum_done", n + 1)
                nc.vector.reciprocal(rden[:, p, :], osum[:, p, :, DH]).then_inc(s["rden_done"], 1)
                after(dve, "rden_done", n + 1)
                nc.vector.tensor_tensor(on[:, p, :].rearrange("p (h d) -> p h d", h=H), osum[:, p, :, 0:DH],
                                        rden[:, p, :].rearrange("p (h a) -> p h a", a=1).broadcast_to([P, H, DH]),
                                        ALU.mult).then_inc(s["on_done"], 1)
            norms = []
            if (k := at(slot, S_ST3, first)) is not None:
                n, p = base + k, k % 2
                after(dve, "ff_done", n + 1)
                after(dve, ("z_done", 2), n - 1)
                nc.vector.tensor_tensor(yff[:, p, :], b["psY"][:, D:2 * D], b["bf_all"][:, :], ALU.add).then_inc(s["ff_read"], 1)
                norms.append((n, k, 2, yff[:, p, :]))
            if (k := at(slot, S_ST1, first)) is not None:
                n, p = base + k, k % 2
                after(dve, "wo_done", n + 1)
                after(dve, ("z_done", 0), n - 1)
                nc.vector.tensor_tensor(att[:, p, :], b["psY"][:, 0:D], b["bo_all"][:, :], ALU.add).then_inc(s["att_read"], 1)
                norms.append((n, k, 0, att[:, p, :]))
            if (k := at(slot, S_ST2, first)) is not None:
                after(dve, "x1_done", base + k + 1)
                after(dve, ("z_done", 1), base + k - 1)
                norms.insert(0, (base + k, k, 1, x1[:, k % 4, :]))
            for n, k, which, rows in norms:
                if which != 1:
                    after(dve, ("att_read", "", "ff_read")[which], n + 1)
            if norms:
                statistics(*norms)
            if (k := at(slot, S_Z1, first)) is not None:
                normalise(base + k, k, 0, z1[:, k % 2, :], att[:, k % 2, :])
            if (k := at(slot, S_H2, first)) is not None:
                normalise(base + k, k, 1, h2[:, k % 2, :], x1[:, k % 4, :])
            if (k := at(slot, S_Z3, first)) is not None:
                normalise(base + k, k, 2, z3[:, k % 2, :], yff[:, k % 2, :])

        nc.vector.memset(q_st[R_PROD:P, :, :, :].rearrange("p r h n -> p (r h n)"), 1.0).then_inc(s["cleared"], 1)
        nc.vector.memset(b["psV"][:, :], 0.0)
        dve.wait_ge(frame_in[0], 16 * FRAME_DMAS)
        nc.vector.tensor_copy(k0[0:R_PROD, :], k_st[0:R_PROD, 0, :, WIN]).then_inc(s["first_rows"], 1)
        nc.vector.tensor_copy(q0[0:R_PROD, :], q_st[0:R_PROD, 0, :, 0]).then_inc(s["first_rows"], 1)
        for m in range(LEAD):
            for u in range(2 * NG):
                take_maxima(0, m, u)
            if m % BF == BF - 1:
                find_shifts(0, m)
        bodies(dve, step)

    @block.scalar
    def _(act):
        def key0(f, kf):
            after(act, "shift_step", 6 * f + 6)
            after(act, "gp_done", 2 * f - 6)
            nc.scalar.activation(eglob[:, kf % RING], earg[:, kf % 2], ACT.Exp).then_inc(s["eg_done"], 1)

        def step(slot, i, first, last):
            base = i * BODY
            if main(slot):
                k, g = main(slot)
                n = base + k
                for u in (2 * g, 2 * g + 1):
                    act.wait_ge(s["b_done"], 8 * n + u + 1)
                    if u % 2 == 0:
                        after(act, "pv_done", 4 * n + g - 3)
                    nc.scalar.activation(prob[:, g, 2 * (u % 2):2 * (u % 2) + 2, :, :].rearrange("p h t n -> p (h t n)"),
                                         b["psB"][u % 2][:, :], ACT.Exp).then_inc(s["exp_done"], 1)
            if (k := at(slot, S_OV, first)) is not None and k % BF == BF - 1 and (k < 0 or ahead(k, last)):
                key0(i * RING + (k + LEAD) // BF, (k + LEAD) // BF)
            if (k := at(slot, S_OV, first)) is not None:
                n = base + k
                after(act, "pv_done", 4 * n + 4)
                after(act, "t1_done", n)
                nc.scalar.copy(oslot[:, :, :].rearrange("p g n -> p (g n)"), b["psV"][:, :]).then_inc(s["ov_done"], 1)
            if (k := at(slot, S_T3, first)) is not None:
                n = base + k
                after(act, "t3_done", n + 1)
                after(act, "ff_done", n)
                nc.scalar.copy(h2T[:, :, :].rearrange("p c n -> p (c n)"), b["psX"][:, D:2 * D]).then_inc(s["e3_done"], 1)
            if (k := at(slot, S_T2, first)) is not None:
                n = base + k
                after(act, "t2_done", n + 1)
                after(act, "wo_done", n)
                nc.scalar.copy(oT[:, :, :].rearrange("p c n -> p (c n)"), b["psX"][:, 0:D]).then_inc(s["e2_done"], 1)

        for f in range(LEAD // BF):
            key0(f, f)
        bodies(act, step)

    @block.gpsimd
    def _(pool):
        def rstd(k, i, which):
            n, p = i * BODY + k, k % 2
            after(pool, ("var_done", which), n + 1)
            nc.gpsimd.tensor_tensor(rs[:, which, p:p + 1], ve[:, which, p:p + 1], b["minus_half"][:, 0:1], ALU.pow)\
                .then_inc(s["rstd_done", which], 1)

        def step(slot, i, first, last):
            base = i * BODY
            for which, offset in enumerate((S_RT1, S_RT2, S_RT3)):
                if (k := at(slot, offset, first)) is not None:
                    rstd(k, i, which)
            if (k := at(slot, S_X1, first)) is not None:
                n, p = base + k, k % 2
                pool.wait_ge(x_in[k % 4], (i * 2 + k // 4 + 1) * 16)
                after(pool, ("z_done", 0), n + 1)
                nc.gpsimd.tensor_tensor(x1[:, k % 4, :], z1[:, p, :], xin[:, k % 4, :], ALU.add).then_inc(s["x1_done"], 1)
            if (k := at(slot, S_RES, first)) is not None:
                n, p = base + k, k % 2
                after(pool, ("z_done", 2), n + 1)
                pool.wait_ge(out_st[p], (i * (BODY // 2) + k // 2 + 1) * 16)
                nc.gpsimd.tensor_tensor(res[:, p, :], z3[:, p, :], x1[:, k % 4, :], ALU.add).then_inc(s["res_done"], 1)
            if (k := at(slot, S_T1, first)) is not None:
                n, p = base + k, k % 2
                after(pool, "eg_done", i * RING + k // BF + 1)
                after(pool, "osum_done", n - 1)
                nc.gpsimd.tensor_tensor(
                    gpart[:, p], v0_all[:, :, :],
                    eglob[:, k // BF % RING, k % BF, :].rearrange("p (h a) -> p h a", a=1).broadcast_to([P, H, DV]),
                    ALU.mult).then_inc(s["gp_done"], 1)
            if main(slot):
                k, g = main(slot)
                n = base + k
                after(pool, "exp_done", 8 * n + 2 * g + 2)
                apart(pool)
                nc.gpsimd.affine_select(out=prob[:, g, :, 0, :], in_=prob[:, g, :, 0, :], pattern=[[0, 4], [-1, P]],
                                        compare_op=ALU.is_ge, fill=0.0, base=0, channel_multiplier=1)\
                    .then_inc(s["sel_done"], 1)
                nc.gpsimd.affine_select(out=prob[:, g, :, 1, :], in_=prob[:, g, :, 1, :], pattern=[[0, 4], [1, P]],
                                        compare_op=ALU.is_ge, fill=0.0, base=0, channel_multiplier=-1)\
                    .then_inc(s["sel_done"], 1)

        pool.wait_ge(v0_in, 16)
        bodies(pool, step)


def stage3(nc, own, b):
    def sb(name, shape, dt=F32):
        return own.enter_context(nc.sbuf_tensor(name, shape, dt))

    v_all = sb("v_all", [P, NT + 1, H * DV])
    tile_max = sb("tile_max", [P, H])
    all_max = sb("all_max", [P, H])
    e0 = sb("e0", [P, NT + 1, H])
    own_head = sb("own_head", [H, H, DV])
    od = sb("od", [H, DV])
    rd = sb("rd", [H, 1])
    diag = sb("diag", [H, D])
    one_row = sb("one_row", [H, 1])
    col = sb("col", [P, 2, DC])
    row = sb("row", [1, 6, D])
    xrow = sb("xrow", [1, D])
    st, mv = sb("st_row", [1, 3, 6]), sb("mv_row", [1, 3, 2])
    ve, rs = sb("ve_row", [1, 3]), sb("rs_row", [1, 3])
    s = {n: own.enter_context(nc.semaphore(n)) for n in (
        "v_all_in", "xrow_in", "row_st", "step0", "max_done", "all_max_done", "less_done", "e0_done",
        "pv0_done", "diag_done", "col_done", "col_copied", "row_done", "var0_done", "rstd0_done")}
    block = own.enter_context(nc.Block())

    @block.sync
    def _(sp):
        sp.dma_start(v_all[:, :, :], b["v_rows"].rearrange("(t p) n -> p t n", p=P)).then_inc(s["v_all_in"], 16)
        sp.dma_start(xrow[:, :], b["x"][0, 0:1, :]).then_inc(s["xrow_in"], 16)
        sp.wait_ge(s["row_done"], 3)
        sp.dma_start(b["out"][0, 0:1, :], row[0:1, 5, :]).then_inc(s["row_st"], 16)
        sp.wait_ge(s["row_st"], 16)

    @block.gpsimd
    def _(pool):
        pool.wait_ge(s["max_done"], 1)
        nc.gpsimd.partition_all_reduce(all_max[:, :], tile_max[:, :], P, bass.bass_isa.ReduceOp.max)\
            .then_inc(s["all_max_done"], 1)
        for which in range(3):
            pool.wait_ge(s["var0_done"], which + 1)
            nc.gpsimd.tensor_tensor(rs[0:1, which:which + 1], ve[0:1, which:which + 1], b["minus_half"][0:1, 0:1],
                                    ALU.pow).then_inc(s["rstd0_done"], 1)

    @block.scalar
    def _(act):
        act.wait_ge(s["less_done"], 1)
        nc.scalar.activation(e0[:, :, :], b["s0"][:, :, :], ACT.Exp).then_inc(s["e0_done"], 1)

    @block.tensor
    def _(pe):
        pe.wait_ge(s["e0_done"], 1)
        pe.wait_ge(s["v_all_in"], 16)
        for t in range(NT + 1):
            op = nc.tensor.matmul(b["psB"][0][0:H, 0:H * DV], e0[:, t, :], v_all[:, t, :], start=(t == 0), stop=(t == NT))
        op.then_inc(s["pv0_done"], 1)
        pe.wait_ge(s["diag_done"], 1)
        for c in range(DC):
            op = nc.tensor.matmul(b["psX"][:, c:c + 1], diag[:, c * P:c * P + P], one_row[:, :], start=True, stop=True)
        op.then_inc(s["col_done"], 1)
        for n, (weight, ps) in enumerate(((b["wo"], b["psY"]), (b["mff"], b["psT"]))):
            if n == 1:
                pe.wait_ge(s["row_done"], 2)
                for c in range(DC):
                    op = nc.tensor.matmul(b["psX"][:, c:c + 1], row[0:1, 3, c * P:c * P + P], one_row[0:1, :],
                                          start=True, stop=True)
                op.then_inc(s["col_done"], 1)
            pe.wait_ge(s["col_copied"], n + 1)
            for c in range(DC):
                op = nc.tensor.matmul(ps[0:1, 0:D], col[:, n, c:c + 1], weight[:, c, :], start=(c == 0), stop=(c == DC - 1))
            op.then_inc(s["pv0_done"], 1)

    @block.vector
    def _(dve):
        done = [0]

        def then(op):
            done[0] += 1
            op.then_inc(s["step0"], 1)
            dve.wait_ge(s["step0"], done[0])

        def norm(which, dst, rows, tells=None):
            then(nc.vector.bn_stats(st[0:1, which, :], rows))
            then(nc.vector.bn_aggr(mv[0:1, which, :], st[0:1, which, :]))
            nc.vector.tensor_scalar(ve[0:1, which:which + 1], mv[0:1, which, 1:2], EPS, None, ALU.add)\
                .then_inc(s["var0_done"], 1)
            dve.wait_ge(s["rstd0_done"], which + 1)
            op = nc.vector.tensor_scalar(dst, rows, mv[0:1, which, 0:1], rs[0:1, which:which + 1],
                                         ALU.subtract, ALU.mult)
            if tells:
                op.then_inc(tells, 1)
            else:
                then(op)

        then(nc.vector.memset(b["s0"][0:WIN, 0, :], NEG))
        then(nc.vector.memset(b["s0"][WIN:P, NT, :], NEG))
        then(nc.vector.memset(one_row[:, :], 1.0))
        nc.vector.tensor_reduce(out=tile_max[:, :], in_=b["s0"][:, :, :].rearrange("p t h -> p h t"), axis=AX.X,
                                op=ALU.max).then_inc(s["max_done"], 1)
        dve.wait_ge(s["all_max_done"], 1)
        nc.vector.tensor_tensor(b["s0"][:, :, :], b["s0"][:, :, :],
                                all_max[:, :].rearrange("p (a h) -> p a h", a=1).broadcast_to([P, NT + 1, H]),
                                ALU.subtract).then_inc(s["less_done"], 1)
        dve.wait_ge(s["pv0_done"], 1)
        then(nc.vector.tensor_tensor(own_head[:, :, :], b["psB"][0][0:H, 0:H * DV].rearrange("p (h d) -> p h d", h=H),
                                     b["ident"][0:H, 0:H].rearrange("p (h a) -> p h a", a=1).broadcast_to([H, H, DV]),
                                     ALU.mult))
        then(nc.vector.tensor_reduce(out=od[:, :], in_=own_head[:, :, :].rearrange("p h d -> p d h"), axis=AX.X, op=ALU.add))
        then(nc.vector.reciprocal(rd[:, :], od[:, DH:DV]))
        nc.vector.tensor_scalar(diag[:, :].rearrange("p (h d) -> p h d", h=H), own_head[:, :, 0:DH], rd[:, 0:1], None,
                                ALU.mult).then_inc(s["diag_done"], 1)
        dve.wait_ge(s["col_done"], 1)
        nc.vector.tensor_copy(col[:, 0, :], b["psX"][:, 0:DC]).then_inc(s["col_copied"], 1)
        dve.wait_ge(s["pv0_done"], 2)
        then(nc.vector.tensor_tensor(row[0:1, 0, :], b["psY"][0:1, 0:D], b["bo_all"][0:1, :], ALU.add))
        norm(0, row[0:1, 1, :], row[0:1, 0, :])
        dve.wait_ge(s["xrow_in"], 16)
        nc.vector.tensor_tensor(row[0:1, 2, :], row[0:1, 1, :], xrow[:, :], ALU.add).then_inc(s["row_done"], 1)
        dve.wait_ge(s["row_done"], 1)
        norm(1, row[0:1, 3, :], row[0:1, 2, :], s["row_done"])
        dve.wait_ge(s["col_done"], 2)
        nc.vector.tensor_copy(col[:, 1, :], b["psX"][:, 0:DC]).then_inc(s["col_copied"], 1)
        dve.wait_ge(s["pv0_done"], 3)
        then(nc.vector.tensor_tensor(row[0:1, 0, :], b["psT"][0:1, 0:D], b["bf_all"][0:1, :], ALU.add))
        norm(2, row[0:1, 4, :], row[0:1, 0, :])
        nc.vector.tensor_tensor(row[0:1, 5, :], row[0:1, 4, :], row[0:1, 2, :], ALU.add).then_inc(s["row_done"], 1)


_INS = ["L0_attn_x", "L0_attn_Wq", "L0_attn_bq", "L0_attn_Wk", "L0_attn_bk", "L0_attn_Wv", "L0_attn_bv",
        "L0_attn_Wo", "L0_attn_bo", "L0_ffn_w_freq_real", "L0_ffn_w_freq_imag", "L0_ffn_bias"]


def constants():
    n = np.arange(D)
    angle = 2.0 * np.pi * (np.outer(n, n) % D) / D
    r, c = (np.arange(P) % WIN)[:, None], np.arange(AW)[None, :]
    mask = np.where((c < r) | (c > r + 2 * WIN), NEG, 0.0)
    mask = np.delete(mask, np.s_[WIN:2 * WIN], axis=1)
    krows = np.zeros((3, SP_))
    krows[0, :WIN + 1] = NEG
    krows[0, WIN + S:] = NEG
    krows[1:] = 1.0
    return {"ident": np.eye(P, dtype=np.float32), "mask": mask.astype(np.float32),
            "krows": krows.astype(np.float32),
            "cos": np.cos(angle).astype(np.float32), "sin": np.sin(angle).astype(np.float32)}


def kernel(**inputs):
    import concourse.bacc as _bacc
    from concourse.bass_utils import run_bass_kernel_spmd as _run

    nc = _bacc.Bacc("TRN2", target_bir_lowering=False, num_devices=1)
    arrays, args = {}, []
    for name, a in [(n, inputs[n]) for n in _INS] + list(constants().items()):
        a = np.ascontiguousarray(a)
        arrays[f"in_{name}"] = a
        args.append(nc.dram_tensor(f"in_{name}", a.shape, mybir.dt.from_np(a.dtype), kind="ExternalInput").ap())
    out = nc.dram_tensor("out", (1, S, D), F32, kind="ExternalOutput").ap()
    build(nc, *args, out)
    r = _run(nc, [arrays], core_ids=[0])
    return r.results[0]["out"]
```

```python
from contextlib import ExitStack

import numpy as np

import concourse.bass as bass
from concourse import mybir

F32 = mybir.dt.float32
BF16 = mybir.dt.bfloat16
ALU = mybir.AluOpType
ACT = mybir.ActivationFunctionType
AX = mybir.AxisListType

S, D, H = 4096, 256, 16
DH = D // H
DV = DH + 1
WIN = 64
P = 128
EPS = 1e-5
NEG = -1e30
SCALE = DH ** -0.5
DC = D // P
NT = S // P
SP_ = S + 2 * WIN
C1 = 512
N1 = S // C1
B1 = C1 // P
C2 = 256
NF = S // C2
BF = C2 // P
KF = C2 + 2 * WIN
RING = 4
BODY = RING * BF
OUTS = (16 * (C1 // C2), 16)
FRAME_DMAS = 7
LEAD = 4
AW = 3 * WIN
NG = 4
QPARTS = (0, 0, 0, 1, 1, 2)
KPARTS = (0, 1, 2, 0, 1, 0)
R_PROD = 16 * len(QPARTS)
R_PAD = R_PROD
R_MAX = R_PROD + 1
K_MAXPASS = R_PAD + 1
K_PROB = R_MAX + 2

S_PV = 2
S_OV = NG + 1
S_T1 = 6
S_DIV = 7
S_T2 = 8
S_WO = 9
S_ST1 = 10
S_RT1 = 12
S_Z1 = 13
S_X1 = 13
S_ST2 = 14
S_RT2 = 15
S_H2 = 17
S_T3 = 18
S_FF = 19
S_ST3 = 20
S_RT3 = 21
S_Z3 = 26
S_RES = 27
S_OUT = 29

Q0_MAX = 17
Q0_ALL_MAX = 18
Q0_LESS = 19
Q0_EXP = 20
Q0_PV = 34
Q0_OWN = 35
Q0_SUM = 36
Q0_DIV = 37
assert Q0_DIV < NG * BODY + S_T2


def build(nc, x, Wq, bq, Wk, bk, Wv, bv, Wo, bo, w_re, w_im, ff_bias, ident_d, ident_b_d, mask_d, krows_d,
          cos_d, sin_d,
          nsin_d, own_head_d, out):
    q_parts = nc.dram_tensor("q_parts", [NF, 3, D, C2], BF16, kind="Internal").ap()
    k_parts = nc.dram_tensor("k_parts", [3, D, SP_], BF16, kind="Internal").ap()
    ident_b_d, mask_d, krows_d = (table.bitcast(BF16) for table in (ident_b_d, mask_d, krows_d))
    v_rows = nc.dram_tensor("v_rows", [SP_, H * DV], F32, kind="Internal").ap()

    ctx = ExitStack()
    with ctx:
        def sb(name, shape, dt=F32):
            return ctx.enter_context(nc.sbuf_tensor(name, shape, dt))

        def sem(name):
            return ctx.enter_context(nc.semaphore(name))

        ident = sb("ident", [P, P])
        ident_b = sb("ident_b", [P, P], BF16)
        mask_b = sb("mask_b", [P, 4 * WIN], BF16)
        wq, wk, wo = (sb(n, [P, DC, D]) for n in ("wq", "wk", "wo"))
        wv = sb("wv", [P, DC, D + 2 * H])
        first_bias = sb("first_bias", [P, 2, H])
        mff = sb("mff", [P, DC, D])
        bqk = sb("bqk", [P, 2, DC])
        bv_all = sb("bv_all", [P, D])
        bo_all, bf_all = (sb(n, [P, D]) for n in ("bo_all", "bf_all"))
        wre, wim, cosm, sinm, nsin, grT, giT = (
            sb(n, [P, DC, D]) for n in ("wre", "wim", "cosm", "sinm", "nsin", "grT", "giT"))
        q_st = sb("q_st", [P, RING, H, C2], BF16)
        k_st = sb("k_st", [P, RING, H, KF], BF16)
        frame_in = [sem(f"frame_in{i}") for i in range(RING)]
        qk_out = [sem(f"qk_out{i}") for i in range(4)]
        v_out = [sem(f"v_out{i}") for i in range(2)]
        minus_half = sb("minus_half", [P, B1])
        psA = ctx.enter_context(nc.psum_tensor("psA", [P, 2, 512], F32))
        psB = [ctx.enter_context(nc.psum_tensor(f"psB{i}", [P, 512], F32)) for i in range(2)]
        psV = ctx.enter_context(nc.psum_tensor("psV", [P, 512], F32))
        psT = ctx.enter_context(nc.psum_tensor("psT", [P, 512], F32))
        psX = ctx.enter_context(nc.psum_tensor("psX", [P, 512], F32))
        psY = ctx.enter_context(nc.psum_tensor("psY", [P, 512], F32))

        first_scores = sb("first_scores", [P, NT, 2, H])
        e0 = sb("e0", [P, NT, 32])
        ones = sb("ones", [P, P])
        own_head = sb("own_head", [P, H])
        b = dict(locals())
        with ExitStack() as own:
            stage1(nc, own, b)
        with ExitStack() as own:
            stage2(nc, own, b)


def stage1_stored(eng, b):
    for w in range(2):
        eng.wait_ge(b["v_out"][w], 16 * (N1 // 2 + 1))
    for w in range(4):
        eng.wait_ge(b["qk_out"][w], OUTS[w % 2] * (N1 // 2 + 1))


def load_frame(sp, b, f, r):
    q_src = b["q_parts"][bass.ds(f, 1)].rearrange("a t (d h) n -> (a t) d (h n)", h=H)
    k_src = b["k_parts"][:, :, bass.ds(f * C2, KF)].rearrange("t (d h) n -> (t d) h n", h=H)
    for row, count, t in ((0, 3, 0), (3, 2, 1), (5, 1, 2)):
        sp.dma_start(b["q_st"][DH * row:DH * (row + count), r, :, :].rearrange("p h n -> p (h n)"),
                     q_src[t:t + 1].broadcast_to([count, DH, H * C2])).then_inc(b["frame_in"][r], 16)
    for row, count in ((0, 3), (3, 2), (5, 1)):
        sp.dma_start(b["k_st"][DH * row:DH * (row + count), r, :, :], k_src[0:DH * count]).then_inc(b["frame_in"][r], 16)
    sp.dma_start(b["k_st"][R_PAD:R_MAX + 2, r, :, :],
                 b["krows_d"][:, bass.ds(f * C2, KF)].rearrange("r (a n) -> r a n", a=1)
                 .broadcast_to([3, H, KF])).then_inc(b["frame_in"][r], 16)


def stage1(nc, own, b):
    def sb(name, shape, dt=F32):
        return own.enter_context(nc.sbuf_tensor(name, shape, dt))

    part = sb("part", [P, 2, 2, 3, DC, C1], BF16)
    vrow = sb("vrow", [P, 2, B1, H, DV])
    xc = sb("xc", [P, 2, B1, D])
    hc = sb("hc", [P, 2, B1, D])
    hT = sb("hT", [P, 2, DC, C1])
    full = sb("full", [P, 2, DC, C1])
    left = sb("left", [P, 2, 2, DC, C1])
    w_plain = sb("w_plain", [P, 2, DC + 1, D])
    h0 = full[:, 1, 0, 0:DC * P].rearrange("p (c n) -> p c n", c=DC)
    spare = left[:, 1].rearrange("p w o n -> p (w o n)")
    row0 = spare[:, 0:2 * D].rearrange("p (i n) -> p i n", i=2)
    prod = spare[:, 2 * D:2 * D + 2 * (DC + 1) * D].rearrange("p (i c n) -> p i c n", i=2, c=DC + 1)
    w_first = sb("w_first", [P, DC + 1, 2, H])
    zb = sb("zb", [P, 3 * DC * WIN], BF16)
    zf = sb("zf", [WIN, H * DV])
    st1 = sb("st1", [P, B1, 6])
    mv1 = sb("mv1", [P, B1, 2])
    ve1 = sb("ve1", [P, B1])
    rs1 = sb("rs1", [P, B1])
    CREDIT = {"h_done": 2, "turned": 2, "hT_copied": 1, "part1_done": 2, "left_done": 2,
              "part3_done": 4, "v_done": 8, "v_copied": 4, "gs_copied": 4}
    s = {n: own.enter_context(nc.semaphore(n)) for n in (
        "stats_done", "aggr_done", "var_done", "rstd_done", "h_done", "turned", "hT_copied", "qk_done",
        "v_done", "part1_done", "left_done", "part2_done", "part3_done", "v_copied", "ones_set", "zeros_set", "half_set", "bias_set", "ordered", "h0_set", "rows_done", "row0_set", "prod_done", "first_sum", "first_set",
        "gs_copied", "rows_in", "g_done", "g_copied",
        "ident_in", "re_in", "im_in", "weights_in", "bias_in", "wv_in", "consts_in", "pads_out", "passed")}
    x_in = [own.enter_context(nc.semaphore(f"x_in{i}")) for i in range(2)]
    qk_out, v_out = b["qk_out"], b["v_out"]
    psQK = [[b["psB"][0], b["psB"][1]], [b["psX"], b["psY"]]]
    psG = [[b["psV"], b["psT"]], [b["psX"], b["psY"]]]
    psVV = [b["psB"][0], b["psB"][1], b["psV"], b["psT"]]
    block = own.enter_context(nc.Block())
    PAIRS = N1 // 2

    def after(eng, name, n):
        eng.wait_ge(s[name], n + CREDIT.get(name, 0))

    def apart(eng):
        eng.sem_inc(s["passed"], 1)

    def chunks(eng, body):
        with eng.Fori(0, PAIRS - 1) as i:
            for par in range(2):
                body(i * 2 + par, par, i, False)
        for par in range(2):
            body(N1 - 2 + par, par, PAIRS - 1, True)

    @block.sync
    def _(sp):
        for w in range(4):
            sp.sem_inc(qk_out[w], OUTS[w % 2])
        for w in range(2):
            sp.sem_inc(v_out[w], 16)
        for name, n in CREDIT.items():
            sp.sem_inc(s[name], n)

        def load(c, par):
            after(sp, "h_done", c - 1)
            sp.dma_start(xc[:, par, :, :],
                         b["x"][0, bass.ds(c * C1, C1), :].rearrange("(j p) d -> p j d", p=P)).then_inc(x_in[par], 16)

        def body(c, par, use, last):
            if not last:
                load(c + 2, par)
            elif par == 0:
                for f in (0, 1):
                    load_frame(sp, b, f, f)
            after(sp, "part3_done", c * 2 + 1)
            for i in range(C1 // C2):
                sp.dma_start(b["q_parts"][bass.ds(c * (C1 // C2) + i, 1)].rearrange("a t (o p) n -> p (a t o) n", p=P),
                             part[:, par, 0, :, :, i * C2:(i + 1) * C2].rearrange("p t o n -> p (t o) n"))\
                    .then_inc(qk_out[2 * par], 16)
            after(sp, "part3_done", c * 2 + 2)
            sp.dma_start(b["k_parts"][:, :, bass.ds(c * C1 + WIN, C1)].rearrange("t (o p) n -> p (t o) n", p=P),
                         part[:, par, 1, :, :, :].rearrange("p t o n -> p (t o) n")).then_inc(qk_out[2 * par + 1], 16)
            after(sp, "v_copied", c * B1 + B1)
            sp.dma_start(b["v_rows"][bass.ds(c * C1 + WIN, C1), :].rearrange("(j p) n -> p j n", p=P),
                         vrow[:, par, :, :, :].rearrange("p j h d -> p j (h d)")).then_inc(v_out[par], 16)

        def fetch(dst, src, signal):
            sp.dma_start(dst, src).then_inc(s[signal], 16)

        rows = "(c p) n -> p c n"
        for name, src in (("wre", "w_re"), ("cosm", "cos_d"), ("nsin", "nsin_d"), ("wim", "w_im"), ("sinm", "sin_d")):
            fetch(b[name][:, :, :], b[src].rearrange(rows, p=P), "im_in" if name in ("wim", "sinm") else "re_in")
            if name == "cosm":
                load(0, 0)
        fetch(b["ident"][:, :], b["ident_d"], "ident_in")
        for i, name in enumerate(("bq", "bk")):
            for c in range(DC):
                sp.dma_start(b["bqk"][:, i, c:c + 1], b[name].rearrange("(h d) -> d h", d=DH)[c * DH // DC:(c + 1) * DH // DC],
                             allow_slow_non_contiguous=True).then_inc(s["bias_in"], 16)
        for i, src in enumerate(("Wq", "Wk")):
            fetch(w_plain[:, i, 0:DC, :], b[src].rearrange(rows, p=P), "weights_in")
        fetch(b["wv"][:, :, 0:D], b["Wv"].rearrange(rows, p=P), "wv_in")
        fetch(b["bv_all"][:, :], b["bv"].rearrange("(a n) -> a n", a=1).broadcast_to([P, D]), "wv_in")
        for i, src in enumerate(("bq", "bk")):
            fetch(w_plain[:, i, DC, :], b[src].rearrange("(a n) -> a n", a=1).broadcast_to([P, D]), "rows_in")
        load(1, 1)
        fetch(b["wo"][:, :, :], b["Wo"].rearrange(rows, p=P), "consts_in")
        for dst, src in (("bo_all", "bo"), ("bf_all", "ff_bias")):
            fetch(b[dst][:, :], b[src].rearrange("(a n) -> a n", a=1).broadcast_to([P, D]), "consts_in")
        fetch(b["ident_b"][:, :], b["ident_b_d"], "consts_in")
        fetch(b["own_head"][:, :], b["own_head_d"], "consts_in")
        for i in range(2):
            fetch(b["mask_b"][:, i * 2 * WIN:(i + 1) * 2 * WIN], b["mask_d"], "consts_in")
        fetch(b["q_st"][R_PAD:R_PAD + 1, :, :, :].rearrange("p r h n -> p (r h) n"),
              b["krows_d"][1:2, 0:C2].rearrange("r (a n) -> r a n", a=1).broadcast_to([1, RING * H, C2]), "consts_in")
        sp.wait_ge(s["zeros_set"], 2)
        for at in (0, WIN + S):
            fetch(b["k_parts"][:, :, at:at + WIN].rearrange("t (c p) n -> p (t c) n", p=P),
                  zb[:, :].rearrange("p (t n) -> p t n", n=WIN), "pads_out")
            fetch(b["v_rows"][at:at + WIN, :], zf[:, :], "pads_out")
        sp.wait_ge(s["pads_out"], 16 * 4)
        chunks(sp, body)
        sp.wait_ge(s["consts_in"], 16 * 8)

    @block.vector
    def _(dve):

        def norm(c, par, use):
            dve.wait_ge(x_in[par], use * 16 + 16)
            for j in range(B1):
                nc.vector.bn_stats(st1[:, j, :], xc[:, par, j, :]).then_inc(s["stats_done"], 1)
            for j in range(B1):
                after(dve, "stats_done", c * B1 + j + 1)
                apart(dve)
                nc.vector.bn_aggr(mv1[:, j, :], st1[:, j, :]).then_inc(s["aggr_done"], 1)
            after(dve, "aggr_done", c * B1 + B1)
            nc.vector.tensor_scalar(ve1[:, :], mv1[:, :, 1], EPS, None, ALU.add).then_inc(s["var_done"], 1)
            after(dve, "rstd_done", c + 1)
            after(dve, "turned", c - 1)
            for j in range(B1):
                op = nc.vector.tensor_scalar(hc[:, par, j, :], xc[:, par, j, :], mv1[:, j, 0:1], rs1[:, j:j + 1],
                                             ALU.subtract, ALU.mult)
            op.then_inc(s["h_done"], 1)
            after(dve, "h_done", c + 1)

        def body(c, par, use, last):
            if not (last and par == 1):
                norm(c + 1, 1 - par, use + par)
            for w in range(2):
                after(dve, "part1_done", c * 2 + w + 1)
                after(dve, "part3_done", c * 2 + w - 3)
                nc.vector.tensor_tensor(left[:, par, w], full[:, w], part[:, par, w, 0], ALU.subtract)\
                    .then_inc(s["left_done"], 1)
                after(dve, "left_done", c * 2 + w + 1)
                nc.vector.tensor_copy(part[:, par, w, 1], left[:, par, w]).then_inc(s["part2_done"], 1)
                if w == 0:
                    dve.wait_ge(v_out[par], 16 * use + 16)
                for t in (2 * w, 2 * w + 1):
                    after(dve, "v_done", c * B1 + t + 1)
                    nc.vector.tensor_tensor(
                        vrow[:, par, t, :, 0:DH], psVV[t][:, 0:D].rearrange("p (h d) -> p h d", d=DH),
                        b["bv_all"][:, :].rearrange("p (h d) -> p h d", d=DH), ALU.add).then_inc(s["v_copied"], 1)

        norm(0, 0, 0)
        dve.wait_ge(s["bias_in"], 64)
        nc.vector.tensor_scalar(b["bqk"][:, 0, :], b["bqk"][:, 0, :], SCALE, None, ALU.mult).then_inc(s["bias_set"], 1)
        for i, dst in enumerate((b["grT"], b["giT"])):
            dve.wait_ge(s["g_done"], i + 1)
            for o in range(DC):
                nc.vector.tensor_copy(dst[:, o, :], psG[i][o][:, 0:D]).then_inc(s["g_copied"], 1)
        dve.wait_ge(s["rows_in"], 32)
        dve.wait_ge(s["weights_in"], 32)
        for i in range(2):
            dve.wait_ge(s["rows_done"], i + 1)
            nc.vector.tensor_tensor(row0[:, i, :], psVV[2 + i][:, 0:D], w_plain[:, 1 - i, DC, :], ALU.add)\
                .then_inc(s["row0_set"], 1)
        for i in range(2):
            dve.wait_ge(s["row0_set"], i + 1)
            nc.vector.tensor_tensor(prod[:, i], w_plain[:, i],
                                    row0[:, i, :].rearrange("p (a n) -> p a n", a=1).broadcast_to([P, DC + 1, D]), ALU.mult)\
                .then_inc(s["prod_done"], 1)
        for i in range(2):
            dve.wait_ge(s["prod_done"], i + 1)
            nc.vector.tensor_reduce(out=w_first[:, :, i, :], in_=prod[:, i].rearrange("p c (h e) -> p c h e", h=H),
                                    axis=AX.X, op=ALU.add).then_inc(s["first_sum"], 1)
        dve.wait_ge(s["first_sum"], 2)
        dve.wait_ge(s["wv_in"], 32)
        nc.vector.tensor_scalar(b["wv"][:, :, D:], w_first[:, 0:DC].rearrange("p c a h -> p c (a h)"), SCALE, None, ALU.mult)\
            .then_inc(s["first_set"], 1)
        nc.vector.tensor_scalar(b["first_bias"][:, :, :], w_first[:, DC], SCALE, None, ALU.mult).then_inc(s["first_set"], 1)
        dve.wait_ge(s["wv_in"], 32)
        dve.wait_ge(s["ones_set"], 1)
        chunks(dve, body)

    @block.gpsimd
    def _(pool):
        def rstd(c):
            after(pool, "var_done", c + 1)
            nc.gpsimd.tensor_tensor(rs1[:, :], ve1[:, :], b["minus_half"][:, :], ALU.pow).then_inc(s["rstd_done"], 1)

        def body(c, par, use, last):
            if not (last and par == 1):
                rstd(c + 1)
            for w in range(2):
                after(pool, "part2_done", c * 2 + w + 1)
                nc.gpsimd.tensor_tensor(part[:, par, w, 2], left[:, par, w], part[:, par, w, 1], ALU.subtract)\
                    .then_inc(s["part3_done"], 1)

        nc.gpsimd.memset(b["minus_half"][:, :], -0.5).then_inc(s["half_set"], 1)
        nc.gpsimd.memset(zb[:, :], 0.0).then_inc(s["zeros_set"], 1)
        nc.gpsimd.memset(zf[:, :], 0.0).then_inc(s["zeros_set"], 1)
        ones = vrow[:, :, :, :, DH:DV].rearrange("p a j h d -> p (a j h) d")
        nc.gpsimd.memset(ones, 1.0).then_inc(s["ones_set"], 1)
        pool.wait_ge(s["half_set"], 1)
        rstd(0)
        chunks(pool, body)

    @block.scalar
    def _(act):
        def hT_copy(c, par):
            after(act, "turned", c + 1)
            after(act, "v_done", (c - 1) * B1)
            nc.scalar.copy(hT[:, par, :, :], b["psA"][:, :, :]).then_inc(s["hT_copied"], 1)

        def body(c, par, use, last):
            for w in range(2):
                act.wait_ge(s["qk_done"], c * 2 + w + 1)
                after(act, "left_done", c * 2 + w - 1)
                act.wait_ge(qk_out[2 * par + w], OUTS[w] * use + OUTS[w])
                for o in range(DC):
                    for dst in (full[:, w, o, :], part[:, par, w, 0, o, :]):
                        op = nc.scalar.activation(dst, psQK[w][o][:, :], ACT.Identity, bias=b["bqk"][:, w, o:o + 1],
                                                  scale=(SCALE, 1.0)[w])
                op.then_inc(s["part1_done"], 1)
            if not (last and par == 1):
                hT_copy(c + 1, 1 - par)
            for t in range(B1):
                after(act, "v_copied", c * B1 + t + 1)
                nc.scalar.copy(b["first_scores"][:, bass.ds(c * B1 + t, 1), :, :].rearrange("p j a h -> p (j a h)"),
                               psVV[t][:, D:D + 2 * H]).then_inc(s["gs_copied"], 1)

        act.wait_ge(s["weights_in"], 32)
        for i, dst in enumerate((b["wq"], b["wk"])):
            for c in range(DC):
                nc.scalar.copy(dst[:, c, :].rearrange("p (e h) -> p e h", h=H),
                               w_plain[:, i, c, :].rearrange("p (h e) -> p e h", h=H)).then_inc(s["ordered"], 1)
        hT_copy(0, 0)
        after(act, "hT_copied", 1)
        nc.scalar.copy(h0[:, :, :], hT[:, 0, :, 0:1].broadcast_to([P, DC, P])).then_inc(s["h0_set"], 1)
        act.wait_ge(s["bias_set"], 1)
        act.wait_ge(s["bias_in"], 64)
        chunks(act, body)

    @block.tensor
    def _(pe):
        def turn(c, par):
            after(pe, "h_done", c + 1)
            after(pe, "hT_copied", c)
            for j in range(B1):
                for d in range(DC):
                    op = nc.tensor.transpose(b["psA"][:, d, j * P:(j + 1) * P], hc[:, par, j, d * P:(d + 1) * P],
                                             b["ident"][:, :])
            op.then_inc(s["turned"], 1)

        def body(c, par, use, last):
            after(pe, "hT_copied", c + 1)
            for w, weight in enumerate((b["wq"], b["wk"])):
                after(pe, "part1_done", c * 2 + w - 1)
                if w == 0:
                    for name in ("v_copied", "gs_copied"):
                        after(pe, name, (c - 1) * B1 + 2)
                for o in range(DC):
                    for d in range(DC):
                        op = nc.tensor.matmul(psQK[w][o][:, :], weight[:, d, o * P:(o + 1) * P], hT[:, par, d, :],
                                              start=(d == 0), stop=(d == DC - 1))
                op.then_inc(s["qk_done"], 1)
            if not (last and par == 1):
                turn(c + 1, 1 - par)
            after(pe, "part1_done", c * 2 + 1)
            pe.wait_ge(s["first_set"], 2)
            for t in range(B1):
                if t >= 2:
                    for name in ("v_copied", "gs_copied"):
                        after(pe, name, (c - 1) * B1 + t + 1)
                for d in range(DC):
                    op = nc.tensor.matmul(psVV[t][:, 0:D + 2 * H], hT[:, par, d, t * P:(t + 1) * P], b["wv"][:, d, :],
                                          start=(d == 0), stop=(d == DC - 1))
                op.then_inc(s["v_done"], 1)

        wre, wim, cosm, sinm, nsin = (b[n] for n in ("wre", "wim", "cosm", "sinm", "nsin"))
        for i, (signal, count, w, factors) in enumerate((("re_in", 3, wre, (cosm, nsin)), ("im_in", 2, wim, (sinm, cosm)))):
            pe.wait_ge(s[signal], 16 * count)
            for g in range(2):
                for o in range(DC):
                    for c in range(DC):
                        mm = nc.tensor.matmul(psG[g][o][:, 0:D], w[:, c, o * P:(o + 1) * P], factors[g][:, c, :],
                                              start=(i + c == 0), stop=(i == 1 and c == DC - 1))
                if i == 1:
                    mm.then_inc(s["g_done"], 1)
        pe.wait_ge(s["ident_in"], 16)
        turn(0, 0)
        pe.wait_ge(s["ordered"], 2 * DC)
        pe.wait_ge(s["wv_in"], 32)
        pe.wait_ge(s["g_copied"], 2 * DC)
        pe.wait_ge(s["h0_set"], 1)
        for i in range(2):
            for d in range(DC):
                op = nc.tensor.matmul(psVV[2 + i][:, 0:D], h0[:, d, :], w_plain[:, 1 - i, d, :], start=(d == 0), stop=(d == DC - 1))
            op.then_inc(s["rows_done"], 1)
        chunks(pe, body)


def stage2(nc, own, b):
    def sb(name, shape, dt=F32):
        return own.enter_context(nc.sbuf_tensor(name, shape, dt))

    q_st, k_st, frame_in = b["q_st"], b["k_st"], b["frame_in"]
    prob = sb("prob", [P, NG, 4, 2, P])
    x1 = sb("x1", [P, 4, D])
    att = sb("att", [P, 2, D])
    z1 = sb("z1", [P, 2, D])
    h2 = sb("h2", [P, 2, D])
    yff = sb("yff", [P, 2, D])
    z3 = sb("z3", [P, 2, D])
    res = sb("res", [P, 2, D])
    oslot = sb("oslot", [P, NG, P])
    v_st = sb("v_st", [P, RING, BF + 1, H, DV])
    v0_all = sb("v0_all", [P, H, DV])
    nmax = sb("nmax", [P, 2, BF, H])
    gsc = sb("gsc", [P, 2, BF, H])
    ngsc = sb("ngsc", [P, BF, H])
    nshift = sb("nshift", [P, BF, H])
    hilo = sb("hilo", [P, 2, BF, 2, H], BF16)
    shift = sb("shift", [P, BF, H])
    earg = sb("earg", [P, 2, BF, H])
    eglob = sb("eglob", [P, RING, BF, H])
    shiftT = sb("shiftT", [2 * H, 2, C2], BF16)
    gpart = sb("gpart", [P, 2, H, DV])
    osum = sb("osum", [P, 2, H, DV])
    rden = sb("rden", [P, 2, H])
    on = sb("on", [P, 2, D])
    oT = sb("oT", [P, DC, P])
    xin = sb("xin", [P, 4, D])
    h2T = sb("h2T", [P, DC, P])
    st = sb("st", [P, 3, 2, 6])
    mv = sb("mv", [P, 3, 2, 2])
    ve = sb("ve", [P, 3, 2])
    rs = sb("rs", [P, 3, 2])

    tile_max = sb("tile_max", [P, H])
    all_max = sb("all_max", [P, H])
    q0_own = sb("q0_own", [P, H, DV])
    TILES = -(-NT // 3)
    v_all = [k_st[:, r, :, :].rearrange("p h n -> p (h n)").bitcast(F32)[:, 0:min(TILES, NT - r * TILES) * H * DV]
             for r in range(3)]

    CREDIT = {"a_read": 2, "exp_done": 2, "pv_done": 4, "ov_done": 1, "t1_done": 1, "osum_done": 2,
              "e2_done": 1, "e3_done": 3, "wo_done": 1, "ff_done": 1, "att_read": 1, "ff_read": 3,
              "eg_done": 2, "gp_done": 8, ("z_done", 0): 2, ("z_done", 1): 2, ("z_done", 2): 2}
    s = {n: own.enter_context(nc.semaphore(n)) for n in (
        "a_done",
        "a_read",
        "shift_step",
        "shT_done",
        "eg_done",
        "b_done",
        "exp_done",
        "sel_done",
        "pv_done",
        "ov_done",
        "t1_done",
        "gp_done",
        "osum_done",
        "rden_done", "on_done",
        "t2_done",
        "e2_done",
        "wo_done",
        "att_read",
        "x1_done",
        "t3_done",
        "e3_done",
        "ff_done",
        "ff_read",
        "res_done",
        "m_done",
        "m_set",
        "q0_max",
        "q0_all_max",
        "q0_less",
        "q0_exp",
        "q0_pv",
        "q0_own",
        "q0_sum",
        "q0_set",
        "q0_scores", "v_all_in", "passed")}
    for n in ("stat_done", "aggr_done", "var_done", "rstd_done", "z_done"):
        for which in range(3):
            s[n, which] = own.enter_context(nc.semaphore(f"{n}{which}"))
    v_in = [own.enter_context(nc.semaphore(f"v_in{i}")) for i in range(RING)]
    x_in = [own.enter_context(nc.semaphore(f"xblock_in{i}")) for i in range(4)]
    shift_in = [own.enter_context(nc.semaphore(f"shift_in{i}")) for i in range(2)]
    out_st = [own.enter_context(nc.semaphore(f"out_st{i}")) for i in range(2)]
    v0_in = own.enter_context(nc.semaphore("v0_in"))
    block = own.enter_context(nc.Block())
    BODIES = NT // BODY
    SLOTS = NG * BODY

    def after(eng, name, n):
        eng.wait_ge(s[name], n + CREDIT.get(name, 0))

    def apart(eng):
        eng.sem_inc(s["passed"], 1)

    def bodies(eng, step):
        for slot in range(SLOTS):
            step(slot, 0, True, False)
        with eng.Fori(1, BODIES - 1) as i:
            for slot in range(SLOTS):
                step(slot, i, False, False)
        for slot in range(SLOTS + S_OUT + 1):
            step(slot, BODIES - 1, False, True)

    def main(slot):
        return divmod(slot, NG) if slot < SLOTS else None

    def at(slot, offset, first, last):
        k, rest = divmod(slot - offset, NG)
        return k if rest == 0 and k < BODY + (last and offset >= S_T2) and (k >= 0 or not first) else None

    def before(k, mine, other, last):
        n = (NG * k + mine - other) // NG + 1
        return min(n, BODY + 1) if last else n

    def ahead(k, last):
        return not last or k + LEAD < BODY

    def late(slot, last):
        return last and slot >= NG * (BODY - LEAD)

    def residuals(eng, compute, slot, i, first, last):
        base = i * BODY
        if (k := at(slot, S_X1, first, last)) is not None:
            n, p = base + k, k % 2
            eng.wait_ge(x_in[k % 4], (i * 2 + k // 4 + 1) * 16)
            after(eng, ("z_done", 0), n + 1)
            if late(slot, last):
                after(eng, "x1_done", n)
                after(eng, "res_done", n - 3)
            compute.tensor_tensor(x1[:, k % 4, :], z1[:, p, :], xin[:, k % 4, :], ALU.add).then_inc(s["x1_done"], 1)
        if (k := at(slot, S_RES, first, last)) is not None:
            n, p = base + k, k % 2
            after(eng, ("z_done", 2), n + 1)
            eng.wait_ge(out_st[p], (i * (BODY // 2) + k // 2 + 1) * 16)
            if late(slot, last):
                after(eng, "res_done", n)
            compute.tensor_tensor(res[:, p, :], z3[:, p, :], x1[:, k % 4, :], ALU.add).then_inc(s["res_done"], 1)

    @block.sync
    def _(sp):
        for name, n in CREDIT.items():
            sp.sem_inc(s[name], n)
        for i in range(2):
            sp.sem_inc(shift_in[i], 32)
            sp.sem_inc(out_st[i], 16)

        def load_v(f, r):
            sp.dma_start(v_st[:, r, :, :, :].rearrange("p t h d -> p t (h d)"),
                         b["v_rows"][bass.ds(f * C2, (BF + 1) * P), :].rearrange("(t p) n -> p t n", p=P))\
                .then_inc(v_in[r], 16)

        def load_x(n, k):
            sp.dma_start(xin[:, k % 4, :], b["x"][0, bass.ds(n * P, P), :]).then_inc(x_in[k % 4], 16)

        def place_shifts(i, kf):
            after(sp, "shT_done", i * RING + kf + 1)
            for part in range(2):
                sp.dma_start(q_st[R_MAX + part:R_MAX + part + 1, kf % RING, :, :],
                             shiftT[part * H:part * H + H, kf % 2, :]).then_inc(shift_in[kf % 2], 16)

        def step(slot, i, first, last):
            base = i * BODY
            if main(slot):
                k, g = main(slot)
                if k % 2 == 0 and g == 2:
                    if ahead(k, last) or k == LEAD:
                        place_shifts(i, (k + LEAD) // BF - 1)
            k = at(slot, S_OV + 1, first, last)
            if k is not None and k % BF == BF - 1 and (not last or k < 0):
                after(sp, "b_done", 8 * (base + k) + 8)
                load_frame(sp, b, (i + 1) * RING + k // BF, k // BF % RING)
                after(sp, "pv_done", 4 * (base + k) + 4)
                load_v((i + 1) * RING + k // BF, k // BF % RING)
            elif k in (1, 3, 5) and last:
                r = k // BF
                after(sp, "b_done", 8 * (base + k) + 8)
                sp.dma_start(v_all[r].rearrange("p (t n) -> p t n", n=H * DV),
                             b["v_rows"][WIN + r * TILES * P:WIN + min(NT, (r + 1) * TILES) * P, :].rearrange("(t p) n -> p t n", p=P))\
                    .then_inc(s["v_all_in"], 16)
            k = at(slot, S_X1 + 1, first, last)
            if k is not None and (not last or k + 4 <= BODY):
                after(sp, "x1_done", base + k + 1)
                load_x(0 if last and k + 4 == BODY else base + k + 4, k)
            k = at(slot, S_OUT, first, last)
            if k is not None:
                after(sp, "res_done", base + k + 1)
                if k < BODY:
                    sp.dma_start(b["out"][0, bass.ds((base + k) * P, P), :], res[:, k % 2, :]).then_inc(out_st[k % 2], 16)
                else:
                    sp.dma_start(b["out"][0, 0:1, :], res[0:1, k % 2, :]).then_inc(out_st[k % 2], 16)

        sp.dma_start(v0_all[:, :, :].rearrange("p h d -> p (h d)"),
                     b["v_rows"][WIN:WIN + 1, :].broadcast_to([P, H * DV])).then_inc(v0_in, 16)
        load_frame(sp, b, 2, 2)
        for f in range(RING):
            load_v(f, f)
            load_x(f, f)
        place_shifts(0, 0)
        load_frame(sp, b, 3, 3)
        stage1_stored(sp, b)
        bodies(sp, step)
        sp.wait_ge(out_st[0], 16 * (NT // 2 + 2))
        sp.wait_ge(out_st[1], 16 * (NT // 2 + 1))

    @block.tensor
    def _(pe):
        def maxima(i, km, u):
            m, use, bank = i * BODY + km, i + km // BODY, u % 2
            r, j = km // BF % RING, km % BF
            after(pe, "a_read", 8 * m + u - 1)
            if u == 0:
                pe.wait_ge(frame_in[r], 16 * FRAME_DMAS * (use + 1))
            for hh in range(2):
                h = 2 * u + hh
                for t in range(2):
                    c = j * P + t * WIN
                    op = nc.tensor.matmul(b["psA"][t * WIN:t * WIN + WIN, bank, hh * AW:hh * AW + AW],
                                          q_st[0:K_MAXPASS, r, h, c:c + WIN], k_st[0:K_MAXPASS, r, h, c:c + AW],
                                          start=(hh == 0), stop=False, skip_group_check=True)
            edges = b["psA"][:, bank, 0:2 * AW].rearrange("p (h e n) -> p h e n", h=2, n=WIN)[:, :, 0:3:2, :]
            op = nc.tensor.matmul(edges, b["ident_b"][:, :], b["mask_b"][:, :], start=False, stop=True,
                                  skip_group_check=True)
            if u == 5 and km % BF == 0 and km > 0:
                op = turn_shifts(i, km)
            op.then_inc(s["a_done"], 1)

        def turn_shifts(i, km):
            kf = km // BF - 1
            after(pe, "shift_step", 6 * (i * RING + kf) + 4)
            for j in range(BF):
                op = nc.tensor.transpose(
                    b["psA"][0:2 * H, 1, 2 * AW + j * WIN:2 * AW + (j + 1) * WIN].bitcast(BF16),
                    hilo[:, kf % 2, j, :, :].rearrange("p a h -> p (a h)"), b["ident_b"][:, :])
            return op

        def scores(n, k, u):
            r, j = k // BF % RING, k % BF
            after(pe, "exp_done", 8 * n + u - 1)
            for hh in range(2):
                for t in range(2):
                    c = (hh * 2 + t) * P
                    op = nc.tensor.matmul(b["psB"][u % 2][:, c:c + P],
                                          k_st[0:K_PROB, r, 2 * u + hh, (j + t) * P:(j + t + 1) * P],
                                          q_st[0:K_PROB, r, 2 * u + hh, j * P:j * P + P], start=True, stop=True)
            op.then_inc(s["b_done"], 1)

        def values(n, k, g):
            r, j = k // BF % RING, k % BF
            after(pe, "sel_done", 8 * n + 2 * g + 2)
            if g == 0:
                after(pe, "ov_done", n)
            for t in range(2):
                for hq in range(4):
                    op = nc.tensor.matmul(b["psV"][32 * hq:32 * hq + DV, g * P:g * P + P], v_st[:, r, j + t, 4 * g + hq, :],
                                          prob[:, g, hq, t, :], start=(t == 0), stop=(t == 1), skip_group_check=True)
            op.then_inc(s["pv_done"], 1)

        def step(slot, i, first, last):
            base = i * BODY
            if main(slot):
                k, g = main(slot)
                n = base + k
                if ahead(k, last):
                    maxima(i, k + LEAD, 2 * g)
                elif k == LEAD and g == 2:
                    after(pe, "a_read", 8 * NT)
                    turn_shifts(i, k + LEAD).then_inc(s["a_done"], 1)
                if g == 0 and k % BF == 0:
                    pe.wait_ge(shift_in[k // BF % 2], (i * (RING // 2) + k // BF // 2 + 2) * 32)
                    pe.wait_ge(v_in[k // BF], 16 * (i + 1))
                scores(n, k, 2 * g)
                if ahead(k, last):
                    maxima(i, k + LEAD, 2 * g + 1)
                scores(n, k, 2 * g + 1)
            if slot - S_PV < SLOTS and not (first and slot < S_PV):
                k, g = divmod(slot - S_PV, NG)
                values(base + k, k, g)
            if (k := at(slot, S_T3, first, last)) is not None:
                n = base + k
                after(pe, ("z_done", 1), n + 1)
                after(pe, "e3_done", n)
                after(pe, "e2_done", base + before(k, S_T3, S_T2, last))
                for c in range(DC):
                    op = nc.tensor.transpose(b["psX"][:, D + c * P:D + c * P + P], h2[:, k % 2, c * P:c * P + P], b["ident"][:, :])
                op.then_inc(s["t3_done"], 1)
            if (k := at(slot, S_FF, first, last)) is not None:
                n = base + k
                after(pe, "e3_done", n + 1)
                after(pe, "ff_read", n)
                after(pe, "att_read", base + before(k, S_FF, S_WO, last))
                for c in range(DC):
                    op = nc.tensor.matmul(b["psY"][:, D:2 * D], h2T[:, c, :], b["mff"][:, c, :], start=(c == 0), stop=(c == DC - 1))
                op.then_inc(s["ff_done"], 1)
            if (k := at(slot, S_T1, first, last)) is not None:
                n = base + k
                after(pe, "ov_done", n + 1)
                after(pe, "osum_done", n)
                for g in range(NG):
                    op = nc.tensor.transpose(b["psT"][:, g * P:g * P + P], oslot[:, g, :], b["ident"][:, :])
                op.then_inc(s["t1_done"], 1)
            if (k := at(slot, S_T2, first, last)) is not None:
                n = base + k
                after(pe, "on_done", n + 1)
                after(pe, "e2_done", n)
                after(pe, "e3_done", base + before(k, S_T2, S_T3, last))
                for c in range(DC):
                    op = nc.tensor.transpose(b["psX"][:, c * P:c * P + P], on[:, k % 2, c * P:c * P + P], b["ident"][:, :])
                op.then_inc(s["t2_done"], 1)
            if last and slot == Q0_PV:
                after(pe, "a_read", 8 * NT)
                pe.wait_ge(s["q0_exp"], 1)
                pe.wait_ge(s["v_all_in"], 16 * 3)
                for t in range(NT):
                    q = t % 4
                    op = nc.tensor.matmul(b["psA"][32 * q:32 * q + 32, 0, 0:H * DV], b["e0"][:, t, :],
                                          v_all[t // TILES][:, t % TILES * H * DV:(t % TILES + 1) * H * DV],
                                          start=(t < 4), stop=(t + 4 >= NT), skip_group_check=True)
                op.then_inc(s["q0_pv"], 1)
            if last and slot == Q0_SUM:
                after(pe, "shT_done", NF)
                pe.wait_ge(s["q0_own"], 1)
                pe.wait_ge(s["q0_set"], 2)
                nc.tensor.matmul(b["psA"][:, 1, 0:H * DV], b["ones"][:, :], q0_own[:, :, :].rearrange("p h d -> p (h d)"),
                                 start=True, stop=True).then_inc(s["q0_sum"], 1)
            if (k := at(slot, S_WO, first, last)) is not None:
                n = base + k
                after(pe, "e2_done", n + 1)
                after(pe, "att_read", n)
                after(pe, "ff_read", base + before(k, S_WO, S_FF, last))
                for c in range(DC):
                    op = nc.tensor.matmul(b["psY"][:, 0:D], oT[:, c, :], b["wo"][:, c, :], start=(c == 0), stop=(c == DC - 1))
                op.then_inc(s["wo_done"], 1)

        terms = [(o, i, c) for o in range(DC) for i in range(2) for c in range(DC)]
        for m in range(LEAD):
            for u in range(2 * NG):
                maxima(0, m, u)
                if m == 0:
                    o, i, c = terms[u]
                    g, f = ((b["grT"], b["cosm"]), (b["giT"], b["nsin"]))[i]
                    mm = nc.tensor.matmul(b["psX"][:, o * D:(o + 1) * D], g[:, c, o * P:(o + 1) * P], f[:, c, :],
                                          start=(i + c == 0), stop=(i == 1 and c == DC - 1))
            if m == 0:
                mm.then_inc(s["m_done"], 1)
        pe.wait_ge(s["m_set"], 1)
        bodies(pe, step)

    @block.vector
    def _(dve):
        def take_maxima(i, km, u):
            m, j, fp, bank = i * BODY + km, km % BF, km // BF % 2, u % 2
            after(dve, "a_done", 8 * m + u + 1)
            if u == 0:
                nc.vector.tensor_tensor(gsc[:, fp, j, :], b["first_scores"][:, bass.ds(m, 1), 0, :].rearrange("p a h -> p (a h)"),
                                        b["first_bias"][:, 0, :], ALU.add)
            if u == 5 and km % BF == 0 and km > 0:
                copy_shifts(i, km)
            nc.vector.tensor_reduce(out=nmax[:, fp, j, 2 * u:2 * u + 2],
                                    in_=b["psA"][:, bank, 0:2 * AW].rearrange("p (h k) -> p h k", h=2),
                                    axis=AX.X, op=ALU.max, negate=True).then_inc(s["a_read"], 1)

        def copy_shifts(i, km):
            kf = km // BF - 1
            dve.wait_ge(shift_in[kf % 2], (i * (RING // 2) + kf // 2 + 1) * 32)
            return nc.vector.tensor_copy(shiftT[:, kf % 2, :], b["psA"][0:2 * H, 1, 2 * AW:512].bitcast(BF16))\
                .then_inc(s["shT_done"], 1)

        def find_shifts(i, km):
            f, fp = i * RING + km // BF, km // BF % 2
            after(dve, "a_read", 8 * (i * BODY + km) + 8)
            nc.vector.tensor_scalar(ngsc[:, :, :], gsc[:, fp], -1.0, None, ALU.mult).then_inc(s["shift_step"], 1)
            after(dve, "shift_step", 6 * f + 1)
            nc.vector.tensor_tensor(nshift[:, :, :], nmax[:, fp], ngsc[:, :, :], ALU.min).then_inc(s["shift_step"], 1)
            after(dve, "shift_step", 6 * f + 2)
            nc.vector.tensor_copy(hilo[:, fp, :, 0, :], nshift[:, :, :]).then_inc(s["shift_step"], 1)
            after(dve, "shift_step", 6 * f + 3)
            nc.vector.tensor_tensor(hilo[:, fp, :, 1, :], nshift[:, :, :], hilo[:, fp, :, 0, :], ALU.subtract)\
                .then_inc(s["shift_step"], 1)
            after(dve, "shift_step", 6 * f + 4)
            nc.vector.tensor_tensor(shift[:, :, :], hilo[:, fp, :, 0, :], hilo[:, fp, :, 1, :], ALU.add)\
                .then_inc(s["shift_step"], 1)
            after(dve, "shift_step", 6 * f + 5)
            after(dve, "eg_done", f - 1)
            nc.vector.tensor_tensor(earg[:, fp], gsc[:, fp], shift[:, :, :], ALU.add).then_inc(s["shift_step"], 1)

        def statistics(*norms):
            for n, k, which, rows in norms:
                nc.vector.bn_stats(st[:, which, k % 2, :], rows).then_inc(s["stat_done", which], 1)
            for n, k, which, rows in norms:
                after(dve, ("stat_done", which), n + 1)
                apart(dve)
                nc.vector.bn_aggr(mv[:, which, k % 2, :], st[:, which, k % 2, :]).then_inc(s["aggr_done", which], 1)
            for n, k, which, rows in norms:
                after(dve, ("aggr_done", which), n + 1)
                nc.vector.tensor_scalar(ve[:, which, k % 2:k % 2 + 1], mv[:, which, k % 2, 1:2], EPS, None, ALU.add)\
                    .then_inc(s["var_done", which], 1)

        def normalise(n, k, which, dst, rows):
            p = k % 2
            after(dve, ("rstd_done", which), n + 1)
            nc.vector.tensor_scalar(dst, rows, mv[:, which, p, 0:1], rs[:, which, p:p + 1], ALU.subtract, ALU.mult)\
                .then_inc(s["z_done", which], 1)

        def step(slot, i, first, last):
            base = i * BODY
            if main(slot):
                k, g = main(slot)
                if ahead(k, last):
                    take_maxima(i, k + LEAD, 2 * g)
                    take_maxima(i, k + LEAD, 2 * g + 1)
                elif k == LEAD and g == 2:
                    after(dve, "a_done", 8 * NT + 1)
                    copy_shifts(i, k + LEAD)
                if g == 0 and (k - 1 + LEAD) % BF == BF - 1 and not (first and k == 0) and (k == 0 or ahead(k - 1, last)):
                    find_shifts(i, k - 1 + LEAD)
            if (k := at(slot, S_DIV, first, last)) is not None:
                n, p = base + k, k % 2
                after(dve, "t1_done", n + 1)
                after(dve, "gp_done", n + 1)
                nc.vector.tensor_tensor(osum[:, p], b["psT"][:, :].rearrange("p (h d) -> p h d", h=H)[:, :, 0:DV],
                                        gpart[:, p], ALU.add).then_inc(s["osum_done"], 1)
                after(dve, "osum_done", n + 1)
                nc.vector.reciprocal(rden[:, p, :], osum[:, p, :, DH]).then_inc(s["rden_done"], 1)
                after(dve, "rden_done", n + 1)
                nc.vector.tensor_tensor(on[:, p, :].rearrange("p (h d) -> p h d", h=H), osum[:, p, :, 0:DH],
                                        rden[:, p, :].rearrange("p (h a) -> p h a", a=1).broadcast_to([P, H, DH]),
                                        ALU.mult).then_inc(s["on_done"], 1)
            if last and slot == Q0_MAX:
                nc.vector.tensor_tensor(b["first_scores"][:, :, 1, :], b["first_scores"][:, :, 1, :],
                                        b["first_bias"][:, 1:2, :].broadcast_to([P, NT, H]), ALU.add)\
                    .then_inc(s["q0_scores"], 1)
                dve.wait_ge(s["q0_scores"], 1)
                nc.vector.tensor_reduce(out=tile_max[:, :], in_=b["first_scores"][:, :, 1, :].rearrange("p t h -> p h t"),
                                        axis=AX.X, op=ALU.max).then_inc(s["q0_max"], 1)
            if last and slot == Q0_LESS:
                dve.wait_ge(s["q0_all_max"], 1)
                nc.vector.tensor_tensor(b["first_scores"][:, :, 1, :], b["first_scores"][:, :, 1, :],
                                        all_max[:, :].rearrange("p (a h) -> p a h", a=1).broadcast_to([P, NT, H]),
                                        ALU.subtract).then_inc(s["q0_less"], 1)
            if last and slot == Q0_OWN:
                dve.wait_ge(s["q0_pv"], 1)
                nc.vector.tensor_tensor(q0_own[:, :, :], b["psA"][:, 0, 0:H * DV].rearrange("p (h d) -> p h d", h=H),
                                        b["own_head"][:, :].rearrange("p (h a) -> p h a", a=1).broadcast_to([P, H, DV]),
                                        ALU.mult).then_inc(s["q0_own"], 1)
            if last and slot == Q0_DIV:
                p = 0
                dve.wait_ge(s["q0_sum"], 1)
                sums = b["psA"][:, 1, 0:H * DV].rearrange("p (h d) -> p h d", h=H)
                after(dve, "on_done", NT)
                nc.vector.reciprocal(rden[:, p, :], sums[:, :, DH]).then_inc(s["rden_done"], 1)
                after(dve, "rden_done", NT + 1)
                nc.vector.tensor_tensor(on[:, p, :].rearrange("p (h d) -> p h d", h=H), sums[:, :, 0:DH],
                                        rden[:, p, :].rearrange("p (h a) -> p h a", a=1).broadcast_to([P, H, DH]),
                                        ALU.mult).then_inc(s["on_done"], 1)
            norms = []
            if (k := at(slot, S_ST3, first, last)) is not None:
                n, p = base + k, k % 2
                after(dve, "ff_done", n + 1)
                after(dve, ("z_done", 2), n - 1)
                nc.vector.tensor_tensor(yff[:, p, :], b["psY"][:, D:2 * D], b["bf_all"][:, :], ALU.add).then_inc(s["ff_read"], 1)
                norms.append((n, k, 2, yff[:, p, :]))
            if (k := at(slot, S_ST1, first, last)) is not None:
                n, p = base + k, k % 2
                after(dve, "wo_done", n + 1)
                after(dve, ("z_done", 0), n - 1)
                nc.vector.tensor_tensor(att[:, p, :], b["psY"][:, 0:D], b["bo_all"][:, :], ALU.add).then_inc(s["att_read"], 1)
                norms.append((n, k, 0, att[:, p, :]))
            if (k := at(slot, S_ST2, first, last)) is not None:
                after(dve, "x1_done", base + k + 1)
                after(dve, ("z_done", 1), base + k - 1)
                norms.insert(0, (base + k, k, 1, x1[:, k % 4, :]))
            for n, k, which, rows in norms:
                if which != 1:
                    after(dve, ("att_read", "", "ff_read")[which], n + 1)
            if norms:
                statistics(*norms)
            if (k := at(slot, S_Z1, first, last)) is not None:
                normalise(base + k, k, 0, z1[:, k % 2, :], att[:, k % 2, :])
            if (k := at(slot, S_H2, first, last)) is not None:
                normalise(base + k, k, 1, h2[:, k % 2, :], x1[:, k % 4, :])
            if (k := at(slot, S_Z3, first, last)) is not None:
                normalise(base + k, k, 2, z3[:, k % 2, :], yff[:, k % 2, :])
            if late(slot, last):
                residuals(dve, nc.vector, slot, i, first, last)

        nc.vector.memset(b["psV"][:, :], 0.0)
        for m in range(LEAD):
            for u in range(2 * NG):
                take_maxima(0, m, u)
            if m % BF == BF - 1:
                find_shifts(0, m)
        stage1_stored(dve, b)
        bodies(dve, step)

    @block.scalar
    def _(act):
        def key0(f, kf):
            after(act, "shift_step", 6 * f + 6)
            after(act, "gp_done", 2 * f - 6)
            nc.scalar.activation(eglob[:, kf % RING], earg[:, kf % 2], ACT.Exp).then_inc(s["eg_done"], 1)

        def step(slot, i, first, last):
            base = i * BODY
            if main(slot):
                k, g = main(slot)
                n = base + k
                for u in (2 * g, 2 * g + 1):
                    act.wait_ge(s["b_done"], 8 * n + u + 1)
                    if u % 2 == 0:
                        after(act, "pv_done", 4 * n + g - 3)
                    nc.scalar.activation(prob[:, g, 2 * (u % 2):2 * (u % 2) + 2, :, :].rearrange("p h t n -> p (h t n)"),
                                         b["psB"][u % 2][:, :], ACT.Exp).then_inc(s["exp_done"], 1)
            if (k := at(slot, S_OV, first, last)) is not None and k % BF == BF - 1 and (k < 0 or ahead(k, last)):
                key0(i * RING + (k + LEAD) // BF, (k + LEAD) // BF)
            if (k := at(slot, S_OV, first, last)) is not None:
                n = base + k
                after(act, "pv_done", 4 * n + 4)
                after(act, "t1_done", n)
                nc.scalar.copy(oslot[:, :, :].rearrange("p g n -> p (g n)"), b["psV"][:, :]).then_inc(s["ov_done"], 1)
            if last and slot == Q0_EXP:
                act.wait_ge(s["q0_less"], 1)
                act.wait_ge(s["q0_set"], 1)
                nc.scalar.activation(b["e0"][:, :, 0:H], b["first_scores"][:, :, 1, :], ACT.Exp).then_inc(s["q0_exp"], 1)
            if (k := at(slot, S_T3, first, last)) is not None:
                n = base + k
                after(act, "t3_done", n + 1)
                after(act, "ff_done", n)
                nc.scalar.copy(h2T[:, :, :].rearrange("p c n -> p (c n)"), b["psX"][:, D:2 * D]).then_inc(s["e3_done"], 1)
            if (k := at(slot, S_T2, first, last)) is not None:
                n = base + k
                after(act, "t2_done", n + 1)
                after(act, "wo_done", n)
                nc.scalar.copy(oT[:, :, :].rearrange("p c n -> p (c n)"), b["psX"][:, 0:D]).then_inc(s["e2_done"], 1)

        key0(0, 0)
        act.wait_ge(s["m_done"], 1)
        nc.scalar.activation(b["mff"][:, :, :].rearrange("p c n -> p (c n)"), b["psX"][:, :], ACT.Identity,
                             scale=1.0 / D).then_inc(s["m_set"], 1)
        for f in range(1, LEAD // BF):
            key0(f, f)
        stage1_stored(act, b)
        bodies(act, step)

    @block.gpsimd
    def _(pool):
        def rstd(k, i, which):
            n, p = i * BODY + k, k % 2
            after(pool, ("var_done", which), n + 1)
            nc.gpsimd.tensor_tensor(rs[:, which, p:p + 1], ve[:, which, p:p + 1], b["minus_half"][:, 0:1], ALU.pow)\
                .then_inc(s["rstd_done", which], 1)

        def step(slot, i, first, last):
            base = i * BODY
            for which, offset in enumerate((S_RT1, S_RT2, S_RT3)):
                if (k := at(slot, offset, first, last)) is not None:
                    rstd(k, i, which)
            if last and slot == Q0_ALL_MAX:
                pool.wait_ge(s["q0_max"], 1)
                nc.gpsimd.partition_all_reduce(all_max[:, :], tile_max[:, :], P, bass.bass_isa.ReduceOp.max)\
                    .then_inc(s["q0_all_max"], 1)
            if not late(slot, last):
                residuals(pool, nc.gpsimd, slot, i, first, last)
            if (k := at(slot, S_T1, first, last)) is not None:
                n, p = base + k, k % 2
                after(pool, "eg_done", i * RING + k // BF + 1)
                after(pool, "osum_done", n - 1)
                nc.gpsimd.tensor_tensor(
                    gpart[:, p], v0_all[:, :, :],
                    eglob[:, k // BF % RING, k % BF, :].rearrange("p (h a) -> p h a", a=1).broadcast_to([P, H, DV]),
                    ALU.mult).then_inc(s["gp_done"], 1)
            if main(slot):
                k, g = main(slot)
                n = base + k
                after(pool, "exp_done", 8 * n + 2 * g + 2)
                apart(pool)
                nc.gpsimd.affine_select(out=prob[:, g, :, 0, :], in_=prob[:, g, :, 0, :], pattern=[[0, 4], [-1, P]],
                                        compare_op=ALU.is_ge, fill=0.0, base=0, channel_multiplier=1)\
                    .then_inc(s["sel_done"], 1)
                nc.gpsimd.affine_select(out=prob[:, g, :, 1, :], in_=prob[:, g, :, 1, :], pattern=[[0, 4], [1, P]],
                                        compare_op=ALU.is_ge, fill=0.0, base=0, channel_multiplier=-1)\
                    .then_inc(s["sel_done"], 1)

        nc.gpsimd.memset(b["e0"][:, :, :], 0.0).then_inc(s["q0_set"], 1)
        nc.gpsimd.memset(b["ones"][:, :], 1.0).then_inc(s["q0_set"], 1)
        pool.wait_ge(v0_in, 16)
        stage1_stored(pool, b)
        bodies(pool, step)


_INS = ["L0_attn_x", "L0_attn_Wq", "L0_attn_bq", "L0_attn_Wk", "L0_attn_bk", "L0_attn_Wv", "L0_attn_bv",
        "L0_attn_Wo", "L0_attn_bo", "L0_ffn_w_freq_real", "L0_ffn_w_freq_imag", "L0_ffn_bias"]


def constants():
    n = np.arange(D)
    angle = 2.0 * np.pi * (np.outer(n, n) % D) / D
    r, c = (np.arange(P) % WIN)[:, None], np.arange(AW)[None, :]
    mask = np.where((c < r) | (c > r + 2 * WIN), NEG, 0.0)
    mask = np.delete(mask, np.s_[WIN:2 * WIN], axis=1)
    krows = np.zeros((3, SP_))
    krows[0, :WIN + 1] = NEG
    krows[0, WIN + S:] = NEG
    krows[1:] = 1.0

    def bf16(a):
        return (a.astype(np.float32).view(np.uint32) >> 16).astype(np.uint16)

    return {"ident": np.eye(P, dtype=np.float32), "ident_b": bf16(np.eye(P)), "mask": bf16(mask), "krows": bf16(krows),
            "cos": np.cos(angle).astype(np.float32), "sin": np.sin(angle).astype(np.float32),
            "nsin": -np.sin(angle).astype(np.float32), "own_head": np.tile(np.eye(32, H, dtype=np.float32), (P // 32, 1))}


def kernel(**inputs):
    import concourse.bacc as _bacc
    from concourse.bass_utils import run_bass_kernel_spmd as _run

    nc = _bacc.Bacc("TRN2", target_bir_lowering=False, num_devices=1)
    arrays, args = {}, []
    for name, a in [(n, inputs[n]) for n in _INS] + list(constants().items()):
        a = np.ascontiguousarray(a)
        arrays[f"in_{name}"] = a
        args.append(nc.dram_tensor(f"in_{name}", a.shape, mybir.dt.from_np(a.dtype), kind="ExternalInput").ap())
    out = nc.dram_tensor("out", (1, S, D), F32, kind="ExternalOutput").ap()
    build(nc, *args, out)
    r = _run(nc, [arrays], core_ids=[0])
    return r.results[0]["out"]
```
